# Optimizing a Trainium2 kernel written in Bass

```python
import numpy as np
import jax
import jax.numpy as jnp

def _softmax(x, axis=-1):
    return jax.nn.softmax(x, axis=axis)

def _gelu(x):
    return jax.nn.gelu(x, approximate=True)

def _silu(x):
    return jax.nn.silu(x)

def _sigmoid(x):
    return jax.nn.sigmoid(x)

def _layernorm(x, axis=-1, eps=1e-05):
    m = jnp.mean(x, axis=axis, keepdims=True)
    v = jnp.var(x, axis=axis, keepdims=True)
    return (x - m) / jnp.sqrt(v + eps)

def _scatter_add(tgt, idx, src, axis=0):
    return tgt.at[idx].add(src)

def _segment_sum(src, seg, n):
    return jax.ops.segment_sum(src, seg, n)
kernel_name = 'mk_adj_resnorm_d1_adj_r2_570c49'

def setup_inputs(seed: int=0):
    np.random.seed(seed)
    _w = jnp.asarray

    def _rec_inputs():
        import jax
        import jax.numpy as jnp
        _gk = jax.random.key(seed)
        x = -0.0004776 + 1.001 * jax.random.normal(jax.random.fold_in(_gk, 1), (4096, 512), jnp.float32)
        _a = jax.random.bernoulli(jax.random.fold_in(_gk, 2), 0.000488281, (4096, 4096))
        _a = jnp.logical_or(_a, jnp.eye(4096, dtype=bool))
        _af = _a.astype(jnp.float32)
        adj = _af
        return (x, adj)
    x, adj = _rec_inputs()

    def _L0_gnn_setup():
        import jax, jax.numpy as jnp
        import numpy as np
        N, H, E, HEADS = (1500, 512, 10000, 8)
        DK = H // HEADS
        key = jax.random.key(seed)
        k1, k2, k3, k4 = jax.random.split(key, 4)
        inst_feature = jax.random.normal(k1, (N, H), dtype=jnp.float32)
        rel_pair_index = jax.random.randint(k2, (E, 2), 0, N, dtype=jnp.int64)
        agg = jnp.zeros((N, N), dtype=jnp.float32)
        agg = agg.at[rel_pair_index[:, 0], rel_pair_index[:, 1]].set(1.0)
        agg = agg.at[jnp.arange(N), jnp.arange(N)].set(1.0)
        std = float(np.sqrt(2.0 / (H + DK)))
        Wq = jax.random.normal(k3, (H, H), dtype=jnp.float32) * std
        Wk = jax.random.normal(k4, (H, H), dtype=jnp.float32) * std
        bq = jnp.zeros((H,), dtype=jnp.float32)
        bk = jnp.zeros((H,), dtype=jnp.float32)
        return {'inst_feature': inst_feature, 'aggregator_matrix': agg, 'rel_pair_index': rel_pair_index, 'Wq': Wq, 'bq': bq, 'Wk': Wk, 'bk': bk}
    _L0_gnn_all = _L0_gnn_setup()
    _L0_gnn_in = {k: v for k, v in _L0_gnn_all.items() if k in ('rel_pair_index', 'Wq', 'bq', 'Wk', 'bk')}
    del _L0_gnn_all
    return {'x': x, 'adj': adj, 'L0_gnn_rel_pair_index': _L0_gnn_in['rel_pair_index'], 'L0_gnn_Wq': _L0_gnn_in['Wq'], 'L0_gnn_bq': _L0_gnn_in['bq'], 'L0_gnn_Wk': _L0_gnn_in['Wk'], 'L0_gnn_bk': _L0_gnn_in['bk']}

def reference(x, adj, L0_gnn_rel_pair_index, L0_gnn_Wq, L0_gnn_bq, L0_gnn_Wk, L0_gnn_bk):
    import jax
    import jax.numpy as jnp

    def _L0_gnn_ref(inst_feature, aggregator_matrix, rel_pair_index, Wq, bq, Wk, bk):
        import jax, jax.numpy as jnp
        import numpy as np
        N, H, E, HEADS = (1500, 512, 10000, 8)
        DK = H // HEADS
        n = inst_feature.shape[0]
        sub = rel_pair_index[:, 0]
        obj = rel_pair_index[:, 1]
        q = (inst_feature[sub] @ Wq.T + bq).reshape(-1, HEADS, DK)
        k = (inst_feature[obj] @ Wk.T + bk).reshape(-1, HEADS, DK)
        att = ((q * k).sum(-1) / np.sqrt(DK)).T.astype(inst_feature.dtype)
        scores = jnp.zeros((HEADS, n, n), dtype=inst_feature.dtype)
        scores = scores.at[:, sub, obj].set(att)
        mask = (1.0 - aggregator_matrix).astype(bool)
        scores = jnp.where(mask[None], -jnp.inf, scores)
        di = jnp.arange(n)
        scores = scores.at[:, di, di].set(1e-07)
        attn = jax.nn.softmax(scores, axis=2)
        aggregator_factor = attn.sum(axis=0) / HEADS
        return aggregator_factor @ inst_feature
    x = _layernorm(x + _L0_gnn_ref(x, adj, L0_gnn_rel_pair_index, L0_gnn_Wq, L0_gnn_bq, L0_gnn_Wk, L0_gnn_bk), axis=-1)
    return x

_drawn_inputs = setup_inputs


def setup_inputs(seed=0):
    import zlib

    import numpy as np

    out = dict(_drawn_inputs(seed))
    spreads = {'L0_gnn_bq': (0.0, 2.0), 'L0_gnn_bk': (0.0, 2.0)}
    factors = {'L0_gnn_Wq': 64.0, 'L0_gnn_Wk': 64.0}
    for name, (base, spread) in spreads.items():
        noise = np.random.default_rng([zlib.crc32(name.encode()), seed]).standard_normal(out[name].shape)
        drawn = base * np.exp(spread * noise) if base else spread * noise
        out[name] = jnp.asarray(drawn.astype(out[name].dtype))
    for name, factor in factors.items():
        out[name] = (out[name] * factor).astype(out[name].dtype)
    return out
```

```python
from contextlib import ExitStack

import numpy as np
import concourse.bass as bass
from concourse import mybir

ALU = mybir.AluOpType
ACT = mybir.ActivationFunctionType
AX = mybir.AxisListType
F32 = mybir.dt.float32
BF16 = mybir.dt.bfloat16
F16 = mybir.dt.float16
I32 = mybir.dt.int32

P = 128
KB = 4
TC = 4
RAW_BUFS = 4
SLOT_GROUP = 3
SCORE_GROUP = 6
SEL_BUFS = 4
HEADS = 8
STAGE = 16
LN_EPS = 1e-5
DIAG_SCORE = 1e-7
NONE = float(2 ** 20)
LOWEST = -1e38
E_OFF = float(np.exp(np.float32(-DIAG_SCORE)))


def edge_columns(E):
    n = -(-E // P)
    while E % n:
        n += 1
    return n


def build(nc, x, adj_t, adj_diag, pairs, wq_t, bq, wk_t, bk, out, g_table, nd_table, edge_list):
    N, H = x.shape
    E = pairs.shape[0]
    ET = edge_columns(E)
    EP = E // ET
    DK = H // HEADS
    assert ET % STAGE == 0
    HC = H // P
    NT = N // P
    GR = N // (P * KB)
    GC = KB * P
    CH = NT // TC

    with ExitStack() as ctx:
        def sb(name, shape, dt):
            return ctx.enter_context(nc.sbuf_tensor(name, shape, dt))

        def psum(name, shape, dt):
            return ctx.enter_context(nc.psum_tensor(name, shape, dt))

        def sem(name):
            return ctx.enter_context(nc.semaphore(name))

        x_raw = sb("x_raw", [P, 2, TC, H], F32)
        x_scaled = sb("x_scaled", [P, 2, TC, H], F32)
        x_hi = sb("x_hi", [P, NT, H], F16)
        x_lo = sb("x_lo", [P, NT, H], F16)
        row_max = sb("row_max", [P, NT], F32)
        expo = sb("expo", [P, NT], I32)
        expo_dn = sb("expo_dn", [P, NT], I32)
        up = sb("up", [P, NT], F32)
        down = sb("down", [P, NT], F32)
        adj_raw = sb("adj_raw", [P, RAW_BUFS, TC, GC], F32)
        sel = sb("sel", [P, SEL_BUFS, TC, GC], BF16)
        count = sb("count", [P, TC, GC], BF16)
        ones = sb("ones", [P, 1], BF16)
        diag_raw = sb("diag_raw", [P, NT], F32)
        diag = sb("diag", [P, NT], F32)
        z_row = sb("z_row", [P, KB], F32)
        inv_z = sb("inv_z", [P, KB], F32)
        w_off = sb("w_off", [P, KB], F32)
        w_d = sb("w_d", [P, KB], F32)
        w_self = sb("w_self", [P, KB], F32)
        x_row = sb("x_row", [P, KB, H], F32)
        g_row = sb("g_row", [P, KB, H], F32)
        nd_row = sb("nd_row", [P, KB, 2], F32)
        y_row = sb("y_row", [P, KB, H], F32)
        stats = sb("stats", [P, KB, 6], F32)
        mean = sb("mean", [P, KB], F32)
        gap = sb("gap", [P, KB], F32)
        gap_sq = sb("gap_sq", [P, KB], F32)
        var = sb("var", [P, KB], F32)
        sq_sum = sb("sq_sum", [P, KB], F32)
        std = sb("std", [P, KB], F32)
        rstd = sb("rstd", [P, KB], F32)
        shift = sb("shift", [P, KB], F32)
        eps_col = sb("eps_col", [P, 1], F32)

        pair_sb = sb("pair_sb", [EP, ET, 2], I32)
        adj_index = sb("adj_index", [EP, ET], I32)
        index_part = sb("index_part", [EP, 3, ET], I32)
        adj_val = sb("adj_val", [EP, ET], F32)
        off_diag = sb("off_diag", [EP, ET], F32)
        live = sb("live", [EP, ET], F32)
        unit = sb("unit", [EP, ET], F32)
        live_sum = sb("live_sum", [EP, ET], F32)
        live_total = sb("live_total", [EP, 1], BF16)
        before = sb("before", [EP, P], BF16)
        all_ones = sb("all_ones", [EP, P], BF16)
        base_total = sb("base_total", [P, 2], F32)
        place = sb("place", [EP, ET], F32)
        place_i = sb("place_i", [EP, ET], I32)
        slot_f = sb("slot_f", [EP, ET], F32)
        slot = sb("slot", [EP, ET], I32)
        n_i = sb("n_i", [P, 1], I32)
        n_tiles = sb("n_tiles", [P, 1], I32)
        edge_sb = sb("edge_sb", [P, ET, 2], I32)
        seq_i = sb("seq_i", [P, ET], I32)
        seq = sb("seq", [P, ET], F32)
        valid = sb("valid", [P, ET], F32)
        src = sb("src", [P, ET], F32)
        key = sb("key", [P, ET], F32)
        att = sb("att", [P, ET, HEADS], F32)
        row_top = sb("row_top", [P, ET, HEADS], F32)
        twins = sb("twins", [P, ET], F32)
        elders = sb("elders", [P, ET], F32)
        once = sb("once", [P, ET], F32)
        rep = sb("rep", [P, ET], F32)
        p_edge = sb("p_edge", [P, ET, HEADS + 1], F32)
        p_zero = sb("p_zero", [P, ET, HEADS], F32)
        p_diag = sb("p_diag", [P, ET, HEADS], F32)
        row_sum = sb("row_sum", [P, ET, HEADS + 1], F32)
        w_diff = sb("w_diff", [P, ET], F32)
        w_zero = sb("w_zero", [P, ET], F32)
        w_own = sb("w_own", [P, ET], F32)
        out_slot_f = sb("out_slot_f", [P, ET], F32)
        out_slot = sb("out_slot", [P, ET], I32)
        ident = sb("ident", [P, P], F32)
        bq_sb = sb("bq_sb", [P, H], F32)
        bk_sb = sb("bk_sb", [P, H], F32)
        field = sb("field", [P, HEADS + 3], F32)
        field_out = sb("field_out", [P, HEADS + 3], F32)
        head_tmp9 = sb("head_tmp9", [P, HEADS + 1], F32)
        adj_stage = sb("adj_stage", [EP, STAGE], F32)
        pair_stage = sb("pair_stage", [EP, STAGE, 2], I32)
        stage = sb("stage", [EP, STAGE], I32)
        ends = sb("ends", [P, 2], I32)
        row_index = sb("row_index", [P, 1], I32)
        tile_top = sb("tile_top", [P, HEADS + 1], F32)
        tile_cnt = sb("tile_cnt", [P, 2], F32)
        nd = sb("nd", [P, 2], F32)
        n_free = sb("n_free", [P, 1], F32)
        z_head = sb("z_head", [P, HEADS], F32)
        iz_head = sb("iz_head", [P, HEADS], F32)
        head_tmp = sb("head_tmp", [P, 3, HEADS], F32)
        w_edge = sb("w_edge", [P, 2], F32)
        w_tmp = sb("w_tmp", [P, 2], F32)
        fix_stats = sb("fix_stats", [P, 6], F32)
        fix_small = sb("fix_small", [P, 8], F32)

        wq_sb, wk_sb = x_scaled[:, 0], x_scaled[:, 1]
        x_src, x_obj = x_raw[:, 0, 0], x_raw[:, 0, 1]
        x_src_t = x_raw[:, 0, 2].rearrange("p (c e) -> p c e", e=P)
        x_obj_t = x_raw[:, 0, 3].rearrange("p (c e) -> p c e", e=P)
        q_sb, k_sb = x_raw[:, 1, 0], x_raw[:, 1, 1]
        fix, fix_sum = x_raw[:, 1, 2], x_raw[:, 1, 3]
        fix_part, fix_y = q_sb, k_sb
        pair_space = x_scaled[:, 0].rearrange("p t h -> p (t h)")
        pair_att = pair_space[:, 0:(HEADS + 1) * P].rearrange("p (h e) -> p h e", e=P)
        spread_sb = pair_space[:, (HEADS + 1) * P:(HEADS + 4) * P]
        same, younger, apart, pair_out = (pair_space[:, (HEADS + i) * P:(HEADS + i + 1) * P] for i in (4, 5, 6, 7))
        g_src, fix_out = x_scaled[:, 1, 0], x_scaled[:, 1, 1]
        assert HC == TC and H == HC * P

        ps_a = psum("ps_a", [P, 2, H], F32)
        ps_b = psum("ps_b", [P, H], F32)
        ps_g = [psum(f"ps_g{k}", [P, H], F32) for k in range(KB)]
        ps_cnt = psum("ps_cnt", [P, H], F32)

        adj_in = [sem(f"adj_in{b}") for b in range(RAW_BUFS)]
        x_in = [sem(f"x_in{b}") for b in range(2)]
        diag_in = sem("diag_in")
        sel_made = sem("sel_made")
        chunk_counted = sem("chunk_counted")
        sel_used = sem("sel_used")
        scale_made = sem("scale_made")
        scaled_x = sem("scaled_x")
        hi_made = sem("hi_made")
        lo_made = sem("lo_made")
        consts = sem("consts")
        x_step = sem("x_step")
        coef_step = sem("coef_step")
        join_step = sem("join_step")
        rstd_made = sem("rstd_made")
        diag_made = sem("diag_made")
        counted = sem("counted")
        coef_made = sem("coef_made")
        bank_done = sem("bank_done")
        bank_read = sem("bank_read")
        xrow_in = sem("xrow_in")
        xpart_made = sem("xpart_made")
        y_made = sem("y_made")
        stats_made = sem("stats_made")
        mv_made = sem("mv_made")
        std_made = sem("std_made")
        shift_made = sem("shift_made")
        out_made = sem("out_made")
        out_sent = sem("out_sent")
        g_sent = sem("g_sent")

        pairs_in = sem("pairs_in")
        weights_in = sem("weights_in")
        index_step = sem("index_step")
        index_made = sem("index_made")
        adj_val_in = sem("adj_val_in")
        list_cleared = sem("list_cleared")
        tables_made = sem("tables_made")
        cleared = sem("cleared")
        total_made = sem("total_made")
        base_made = sem("base_made")
        slots_made = sem("slots_made")
        listed = sem("listed")
        edges_in = sem("edges_in")
        ends_in = sem("ends_in")
        ends_turned = sem("ends_turned")
        turned_read = sem("turned_read")
        qk_made = sem("qk_made")
        qk_read = sem("qk_read")
        att_made = sem("att_made")
        fields_made = sem("fields_made")
        spread = sem("spread")
        exp_in = sem("exp_in")
        exp_made = sem("exp_made")
        sums_field = sem("sums_field")
        sums_spread = sem("sums_spread")
        nd_sent = sem("nd_sent")
        nd_in = sem("nd_in")
        nd_used = sem("nd_used")
        src_field = sem("src_field")
        src_spread = sem("src_spread")
        own_in = sem("own_in")
        g_src_in = sem("g_src_in")
        obj_in = sem("obj_in")
        pair_ready = sem("pair_ready")
        pair_done = sem("pair_done")
        pair_added = sem("pair_added")
        fix_var = sem("fix_var")
        fix_std = sem("fix_std")
        fixed = sem("fixed")
        weighed = sem("weighed")
        pair_room = sem("pair_room")
        fix_sent = sem("fix_sent")
        staged = sem("staged")

        x_tiles = x.rearrange("(c t p) h -> c p t h", p=P, t=TC)
        adj_chunks = adj_t.rearrange("g p (c t) i -> g c p t i", t=TC)
        x_rows = x.rearrange("(g k p) h -> g p k h", p=P, k=KB)
        out_rows = out.rearrange("(g k p) h -> g p k h", p=P, k=KB)
        nd_rows = nd_table.rearrange("(g k p) c -> g p k c", p=P, k=KB)
        edge_tiles = edge_list.rearrange("(p t) c -> p t c", t=ET)
        adj_flat = adj_t.rearrange("g p t (i o) -> (g p t i) o", o=1)
        g_rows = g_table.rearrange("(g k p) h -> g p k h", p=P, k=KB)

        block = ctx.enter_context(nc.Block())

        @block.sync
        def _(sp):
            def load_adj(g, c, wait):
                b = c % RAW_BUFS
                if wait:
                    sp.wait_ge(chunk_counted, g * CH + c + 1 - RAW_BUFS)
                sp.dma_start(adj_raw[:, b], adj_chunks[g, c]).then_inc(adj_in[b], 16)

            sp.dma_start(pair_sb[:], pairs.rearrange("(p t) c -> p t c", t=ET)).then_inc(pairs_in, 16)
            for c in range(CH):
                if c >= 2:
                    sp.wait_ge(scaled_x, TC * (c - 1))
                sp.dma_start(x_raw[:, c % 2], x_tiles[c]).then_inc(x_in[c % 2], 16)
                load_adj(0, c, c >= RAW_BUFS)
                if c == 0:
                    sp.dma_start(diag_raw[:], adj_diag).then_inc(diag_in, 16)
            sp.dma_start(x_row[:], x_rows[0]).then_inc(xrow_in, 16)
            sp.wait_ge(lo_made, CH)
            sp.dma_start(wq_sb, wq_t.rearrange("(c p) h -> p c h", p=P)).then_inc(weights_in, 16)
            sp.dma_start(wk_sb, wk_t.rearrange("(c p) h -> p c h", p=P)).then_inc(weights_in, 16)
            sp.dma_start(bq_sb[:], bq.partition_broadcast(P)).then_inc(weights_in, 16)
            sp.dma_start(bk_sb[:], bk.partition_broadcast(P)).then_inc(weights_in, 16)
            with sp.Fori(1, GR) as g:
                for c in range(CH):
                    load_adj(g, c, True)
                    if c == 3:
                        sp.wait_ge(y_made, KB * g)
                        sp.dma_start(x_row[:], x_rows[g]).then_inc(xrow_in, 16)

        @block.gpsimd
        def _(pool):
            nc.gpsimd.memset(ones[:], 1.0).then_inc(consts, 1)
            nc.gpsimd.memset(eps_col[:], LN_EPS).then_inc(consts, 1)
            nc.gpsimd.memset(edge_sb[:], 0).then_inc(cleared, 1)
            nc.gpsimd.memset(unit[:], 1.0).then_inc(tables_made, 1)
            nc.gpsimd.memset(all_ones[:], 1.0).then_inc(tables_made, 1)
            nc.gpsimd.memset(before[:], 1.0).then_inc(cleared, 1)
            nc.gpsimd.memset(ident[:], 0.0).then_inc(cleared, 1)
            pool.wait_ge(cleared, 3)
            pool.dma_start(edge_tiles, edge_sb[:]).then_inc(list_cleared, 16)
            nc.gpsimd.affine_select(out=before[:], in_=before[:], compare_op=ALU.is_gt, fill=0.0, base=0,
                                    pattern=[[1, P]], channel_multiplier=-1).then_inc(tables_made, 1)
            nc.gpsimd.affine_select(out=ident[:], in_=ident[:], compare_op=ALU.not_equal, fill=1.0, base=0,
                                    pattern=[[1, P]], channel_multiplier=-1).then_inc(tables_made, 1)
            nc.gpsimd.iota(seq_i[:], pattern=[[P, ET]], base=0, channel_multiplier=1).then_inc(tables_made, 1)
            for c in range(CH):
                pool.wait_ge(hi_made, TC * (c + 1))
                nc.gpsimd.tensor_tensor(x_lo[:, TC * c:TC * (c + 1)], x_scaled[:, c % 2],
                                        x_hi[:, TC * c:TC * (c + 1)], ALU.subtract).then_inc(lo_made, 1)
            pool.sem_inc(att_made, 1)
            pool.sem_inc(nd_used, 1)
            pool.sem_inc(pair_room, 1)
            pool.wait_ge(index_made, 1)
            with pool.Fori(0, ET // STAGE) as r:
                nc.gpsimd.tensor_copy(stage[:], adj_index[:, bass.ds(r * STAGE, STAGE)])
                pool.drain()
                for c in range(STAGE):
                    pool.indirect_dma_start(
                        out=adj_stage[:, c:c + 1], out_offset=None, in_=adj_flat,
                        in_offset=bass.IndirectOffsetOnAxis(ap=stage[:, c:c + 1], axis=0)).then_inc(adj_val_in, 16)
                pool.wait_ge(adj_val_in, 16 * STAGE * r + 16 * STAGE)
                nc.gpsimd.tensor_copy(adj_val[:, bass.ds(r * STAGE, STAGE)], adj_stage[:]).then_inc(staged, 1)
            pool.wait_ge(slots_made, 1)
            pool.wait_ge(list_cleared, 16)
            with pool.Fori(0, ET // STAGE) as r:
                nc.gpsimd.tensor_copy(stage[:], slot[:, bass.ds(r * STAGE, STAGE)])
                nc.gpsimd.tensor_copy(pair_stage[:], pair_sb[:, bass.ds(r * STAGE, STAGE)])
                pool.drain()
                for c in range(STAGE):
                    pool.indirect_dma_start(
                        out=edge_list, out_offset=bass.IndirectOffsetOnAxis(ap=stage[:, c:c + 1], axis=0),
                        in_=pair_stage[:, c], in_offset=None,
                        bounds_check=P * ET - 1, oob_is_err=False).then_inc(listed, 16)
                pool.drain()
            pool.dma_start(edge_sb[:], edge_tiles).then_inc(edges_in, 16)
            pool.wait_ge(edges_in, 16)
            tiles = pool.value_load(n_tiles[0:1, 0:1], min_val=1, max_val=ET)

            def gather(dst, table, end):
                return pool.indirect_dma_start(
                    out=dst, out_offset=None, in_=table,
                    in_offset=bass.IndirectOffsetOnAxis(ap=ends[:, end:end + 1], axis=0))

            with pool.Fori(0, tiles) as a:
                pool.wait_ge(att_made, a + 1)
                nc.gpsimd.tensor_copy(ends[:], edge_sb[:, bass.ds(a, 1)].rearrange("p o c -> p (o c)"))
                pool.drain()
                gather(x_src, x, 0).then_inc(ends_in, 16)
                gather(x_obj, x, 1).then_inc(ends_in, 16)
                pool.drain()
            pool.wait_ge(nd_sent, 16 * GR)
            with pool.Fori(0, tiles) as a:
                pool.wait_ge(nd_used, a + 1)
                nc.gpsimd.tensor_copy(ends[:], edge_sb[:, bass.ds(a, 1)].rearrange("p o c -> p (o c)"))
                pool.drain()
                gather(nd[:], nd_table, 0).then_inc(nd_in, 16)
                pool.drain()
            pool.wait_ge(weighed, 1)
            with pool.Fori(0, tiles) as a:
                nc.gpsimd.tensor_copy(ends[:], edge_sb[:, bass.ds(a, 1)].rearrange("p o c -> p (o c)"))
                pool.drain()
                gather(x_src, x, 0).then_inc(own_in, 16)
                pool.wait_ge(g_sent, 16 * GR)
                gather(g_src, g_table, 0).then_inc(g_src_in, 16)
                pool.drain()
                with pool.Fori(0, tiles) as b:
                    n = a * tiles + b
                    pool.wait_ge(pair_room, n + 1)
                    nc.gpsimd.tensor_copy(ends[:], edge_sb[:, bass.ds(b, 1)].rearrange("p o c -> p (o c)"))
                    pool.drain()
                    gather(x_obj, x, 1).then_inc(obj_in, 16)
                    pool.drain()
                pool.wait_ge(fixed, a + 1)
                nc.gpsimd.tensor_copy(row_index[:], out_slot[:, bass.ds(a, 1)])
                pool.drain()
                pool.wait_ge(out_sent, 16 * GR)
                pool.indirect_dma_start(
                    out=out, out_offset=bass.IndirectOffsetOnAxis(ap=row_index[:], axis=0),
                    in_=fix_out, in_offset=None, bounds_check=N - 1, oob_is_err=False).then_inc(fix_sent, 16)
                pool.drain()
            pool.wait_ge(fix_sent, 16)

        def coefficients(dve, g):
            dve.wait_ge(counted, g + 1)
            if not (isinstance(g, int) and g == 0):
                dve.wait_ge(nd_sent, 16 * g)
                dve.wait_ge(xpart_made, KB * g)
            d = diag[:, bass.ds(g * KB, KB)]
            step = 5 * g
            nc.vector.tensor_copy(nd_row[:, :, 1], d)
            nc.vector.tensor_tensor(nd_row[:, :, 0], ps_cnt[:, 0:KB], d, ALU.subtract).then_inc(coef_step, 1)
            dve.wait_ge(coef_step, step + 1)
            nc.vector.tensor_scalar(z_row[:], nd_row[:, :, 0], E_OFF, 1.0, ALU.mult, ALU.add).then_inc(coef_step, 1)
            dve.wait_ge(coef_step, step + 2)
            nc.vector.reciprocal(inv_z[:], z_row[:]).then_inc(coef_step, 1)
            dve.wait_ge(coef_step, step + 3)
            nc.vector.tensor_scalar(w_off[:], inv_z[:], E_OFF, None, ALU.mult).then_inc(coef_step, 1)
            dve.wait_ge(coef_step, step + 4)
            nc.vector.tensor_tensor(w_d[:], w_off[:], d, ALU.mult).then_inc(coef_step, 1)
            dve.wait_ge(coef_step, step + 5)
            nc.vector.scalar_tensor_tensor(w_self[:], inv_z[:], 1.0, w_d[:], ALU.add,
                                           ALU.subtract).then_inc(coef_made, 1)

        def mix_rows(dve, g):
            for k in range(KB):
                dve.wait_ge(bank_read, KB * g + k + 1)
                dve.wait_ge(xpart_made, KB * g + k + 1)
                if k == 0 and not (isinstance(g, int) and g == 0):
                    dve.wait_ge(out_sent, 16 * g)
                nc.vector.scalar_tensor_tensor(y_row[:, k], g_row[:, k], w_off[:, k:k + 1], x_row[:, k],
                                               ALU.mult, ALU.add).then_inc(y_made, 1)
                dve.wait_ge(y_made, KB * g + k + 1)
                nc.vector.bn_stats(stats[:, k], y_row[:, k]).then_inc(stats_made, 1)
            dve.wait_ge(stats_made, KB * (g + 1))
            nc.vector.tensor_tensor(mean[:], stats[:, :, 1], stats[:, :, 4], ALU.add).then_inc(join_step, 1)
            nc.vector.tensor_tensor(gap[:], stats[:, :, 1], stats[:, :, 4], ALU.subtract).then_inc(join_step, 1)
            nc.vector.tensor_tensor(var[:], stats[:, :, 2], stats[:, :, 5], ALU.add).then_inc(join_step, 1)
            dve.wait_ge(join_step, 4 * g + 2)
            nc.vector.scalar_tensor_tensor(gap_sq[:], gap[:], H / 4.0, gap[:], ALU.mult, ALU.mult).then_inc(join_step, 1)
            dve.wait_ge(join_step, 4 * g + 4)
            nc.vector.tensor_tensor(sq_sum[:], var[:], gap_sq[:], ALU.add).then_inc(mv_made, 1)

        def scale_rows(dve, g):
            dve.wait_ge(std_made, g + 1)
            nc.vector.reciprocal(rstd[:], std[:]).then_inc(rstd_made, 1)
            dve.wait_ge(rstd_made, g + 1)
            nc.vector.scalar_tensor_tensor(shift[:], mean[:], -0.5, rstd[:], ALU.mult,
                                           ALU.mult).then_inc(shift_made, 1)

        def select_chunk(dve, g, c, first):
            b = c % RAW_BUFS
            dve.wait_ge(adj_in[b], (g * (CH // RAW_BUFS) + c // RAW_BUFS + 1) * 16)
            if c >= SEL_BUFS:
                dve.wait_ge(sel_used, g * (CH - 1) + c + 1 - SEL_BUFS)
            elif not first and c == SEL_BUFS - 1:
                dve.wait_ge(bank_done, g * KB)
            elif not first:
                dve.wait_ge(sel_used, (g - 1) * (CH - 1) + c + 1 + CH - SEL_BUFS)
            for t in range(TC):
                last = nc.vector.tensor_scalar(sel[:, c % SEL_BUFS, t], adj_raw[:, b, t], 1.0,
                                               down[:, TC * c + t:TC * c + t + 1],
                                               ALU.is_equal, ALU.mult)
            last.then_inc(sel_made, 1)
            if c == 0:
                if not first:
                    dve.wait_ge(counted, g)
                nc.vector.tensor_scalar(count[:], adj_raw[:, b], 1.0, None, ALU.is_equal).then_inc(chunk_counted, 1)
            else:
                dve.wait_ge(chunk_counted, g * CH + c)
                nc.vector.scalar_tensor_tensor(count[:].rearrange("p t i -> p (t i)"), adj_raw[:, b].rearrange("p t i -> p (t i)"), 1.0,
                                               count[:].rearrange("p t i -> p (t i)"),
                                               ALU.is_equal, ALU.add).then_inc(chunk_counted, 1)

        def scale_x(dve, c):
            dve.wait_ge(x_in[c % 2], 16 * (c // 2 + 1))
            ts = slice(TC * c, TC * (c + 1))
            nc.vector.tensor_reduce(row_max[:, ts], x_raw[:, c % 2], AX.X, ALU.max,
                                    apply_absolute_value=True).then_inc(x_step, 1)
            dve.wait_ge(x_step, 4 * c + 1)
            nc.vector.tensor_scalar(expo[:, ts], row_max[:, ts].bitcast(I32), 23, None,
                                    ALU.logical_shift_right).then_inc(x_step, 1)
            dve.wait_ge(x_step, 4 * c + 2)
            nc.vector.tensor_scalar(expo_dn[:, ts], expo[:, ts], 15.0, -14.0, ALU.max, ALU.add).then_inc(x_step, 1)
            dve.wait_ge(x_step, 4 * c + 3)
            nc.vector.tensor_scalar(expo[:, ts], expo_dn[:, ts], -1.0, 254.0, ALU.mult, ALU.add).then_inc(x_step, 1)
            dve.wait_ge(x_step, 4 * c + 4)
            nc.vector.tensor_scalar(up[:, ts].bitcast(I32), expo[:, ts], 23, None,
                                    ALU.logical_shift_left).then_inc(scale_made, 1)
            nc.vector.tensor_scalar(down[:, ts].bitcast(I32), expo_dn[:, ts], 23, None,
                                    ALU.logical_shift_left).then_inc(scale_made, 1)
            dve.wait_ge(scale_made, 2 * (c + 1))

        def edge_index(dve):
            dve.wait_ge(pairs_in, 16)
            s, o = pair_sb[:, :, 0], pair_sb[:, :, 1]
            lg, lp, lt = GC.bit_length() - 1, P.bit_length() - 1, (NT * GC).bit_length() - 1
            SHR, SHL, AND, OR = ALU.logical_shift_right, ALU.logical_shift_left, ALU.bitwise_and, ALU.bitwise_or
            nc.vector.tensor_scalar(index_part[:, 0], s, lg, lp + lt, SHR, SHL)
            nc.vector.tensor_scalar(index_part[:, 1], o, P - 1, lt, AND, SHL)
            nc.vector.tensor_scalar(index_part[:, 2], o, lp, lg, SHR, SHL)
            nc.vector.tensor_scalar(adj_index[:], s, GC - 1, None, AND)
            nc.vector.tensor_tensor(off_diag[:], s, o, ALU.not_equal)
            for i in range(3):
                dve.drain()
                last = nc.vector.tensor_tensor(adj_index[:], adj_index[:], index_part[:, i], OR)
            last.then_inc(index_made, 1)

        def edge_slots(dve):
            dve.wait_ge(staged, ET // STAGE)
            nc.vector.scalar_tensor_tensor(live[:], adj_val[:], 1.0, off_diag[:], ALU.is_equal, ALU.mult)
            dve.wait_ge(tables_made, 5)
            nc.vector.tensor_copy(seq[:], seq_i[:])
            dve.drain()
            nc.vector.tensor_tensor_scan(live_sum[:], unit[:], live[:], 0.0, ALU.mult, ALU.add)
            dve.drain()
            nc.vector.tensor_copy(live_total[:], live_sum[:, ET - 1:ET]).then_inc(total_made, 1)
            dve.wait_ge(base_made, 1)
            nc.vector.tensor_copy(base_total[:], ps_b[:, 0:2])
            dve.drain()
            nc.vector.scalar_tensor_tensor(place[:], live_sum[:], base_total[0:EP, 0:1], live[:], ALU.add, ALU.subtract)
            nc.vector.tensor_scalar(n_i[:], base_total[:, 1:2], float(P - 1), None, ALU.add)
            nc.vector.tensor_scalar(valid[:], seq[:], base_total[:, 1:2], None, ALU.is_lt)
            dve.drain()
            nc.vector.tensor_copy(place_i[:], place[:])
            nc.vector.tensor_scalar(n_tiles[:], n_i[:], P.bit_length() - 1, None, ALU.logical_shift_right)
            dve.drain()
            nc.vector.tensor_scalar(slot[:], place_i[:], P.bit_length() - 1, None, ALU.logical_shift_right)
            nc.vector.tensor_scalar(n_tiles[:], n_tiles[:], 1.0, None, ALU.max)
            dve.drain()
            nc.vector.tensor_scalar(slot_f[:], slot[:], -float(P * ET - 1), None, ALU.mult)
            dve.drain()
            nc.vector.scalar_tensor_tensor(slot_f[:], place[:], float(ET), slot_f[:], ALU.mult, ALU.add)
            dve.drain()
            nc.vector.scalar_tensor_tensor(slot_f[:], slot_f[:], -NONE, live[:], ALU.add, ALU.mult)
            dve.drain()
            nc.vector.tensor_scalar(slot[:], slot_f[:], NONE, None, ALU.add).then_inc(slots_made, 1)

        def edge_scores(dve, tiles):
            dve.wait_ge(edges_in, 16)
            nc.vector.tensor_copy(src[:], edge_sb[:, :, 0])
            nc.vector.tensor_copy(key[:], edge_sb[:, :, 1])
            nc.vector.memset(att[:], 0.0)
            nc.vector.memset(row_top[:], DIAG_SCORE)
            nc.vector.memset(twins[:], 0.0)
            nc.vector.memset(elders[:], 0.0)
            nc.vector.memset(row_sum[:], 0.0)
            dve.drain()
            nc.vector.scalar_tensor_tensor(src[:], src[:], 1.0, valid[:], ALU.add, ALU.mult)
            dve.drain()
            nc.vector.tensor_scalar(src[:], src[:], -1.0, None, ALU.add)
            dve.drain()
            nc.vector.scalar_tensor_tensor(key[:], src[:], float(N), key[:], ALU.mult, ALU.add)
            dve.wait_ge(weights_in, 64)
            with dve.Fori(0, tiles) as a:
                dve.wait_ge(qk_made, 2 * a + 1)
                nc.vector.tensor_tensor(q_sb, ps_a[:, 0], bq_sb[:], ALU.add)
                dve.wait_ge(qk_made, 2 * a + 2)
                nc.vector.tensor_tensor(k_sb, ps_a[:, 1], bk_sb[:], ALU.add)
                dve.drain()
                nc.vector.tensor_tensor(q_sb, q_sb, k_sb, ALU.mult)
                dve.drain()
                nc.vector.tensor_reduce(tile_top[:, 0:HEADS], q_sb.rearrange("p (h d) -> p h d", h=HEADS), AX.X, ALU.add)
                dve.drain()
                nc.vector.tensor_scalar(att[:, bass.ds(a, 1)].rearrange("p o h -> p (o h)"), tile_top[:, 0:HEADS],
                                        1.0 / float(np.sqrt(DK)), valid[:, bass.ds(a, 1)],
                                        ALU.mult, ALU.mult).then_inc(att_made, 1)

            def one(t, a):
                return t[:, bass.ds(a, 1)]

            def heads(t, a):
                return t[:, bass.ds(a, 1)].rearrange("p o h -> p (o h)")

            dve.drain()
            with dve.Fori(0, tiles) as b:
                nc.vector.tensor_copy(field[:, 0:HEADS], heads(att, b))
                nc.vector.tensor_copy(field[:, HEADS:HEADS + 1], one(src, b))
                nc.vector.tensor_copy(field[:, HEADS + 1:HEADS + 2], one(key, b))
                nc.vector.tensor_copy(field[:, HEADS + 2:HEADS + 3], one(seq, b))
                dve.drain()
                nc.vector.tensor_copy(field_out[:], field[:]).then_inc(fields_made, 1)
                dve.wait_ge(spread, b + 1)
                nc.vector.tensor_copy(spread_sb, ps_b[:, 0:3 * P])
                dve.drain()
                with dve.Fori(0, tiles) as a:
                    nc.vector.tensor_scalar(same, spread_sb[:, 0:P], one(src, a), None, ALU.is_equal)
                    nc.vector.tensor_scalar(younger, spread_sb[:, 2 * P:3 * P], one(seq, a), None, ALU.is_lt)
                    dve.drain()
                    nc.vector.tensor_scalar(apart, same, -LOWEST, LOWEST, ALU.mult, ALU.add)
                    nc.vector.scalar_tensor_tensor(pair_out, spread_sb[:, P:2 * P], one(key, a), younger,
                                                   ALU.is_equal, ALU.mult, accum_out=tile_cnt[:, 0:1])
                    nc.vector.scalar_tensor_tensor(pair_att[:, HEADS], same, 1.0, younger,
                                                   ALU.mult, ALU.mult, accum_out=tile_cnt[:, 1:2])
                    dve.drain()
                    for i in range(2):
                        nc.vector.tensor_tensor(pair_att[:, 4 * i:4 * i + 4], ps_a[:, i].rearrange("p (h e) -> p h e", e=P),
                                                apart.unsqueeze(1).to_broadcast([P, 4, P]), ALU.add)
                    nc.vector.tensor_tensor(one(twins, a), one(twins, a), tile_cnt[:, 0:1], ALU.add)
                    nc.vector.tensor_tensor(one(elders, a), one(elders, a), tile_cnt[:, 1:2], ALU.add)
                    dve.drain()
                    nc.vector.tensor_reduce(tile_top[:, 0:HEADS], pair_att[:, 0:HEADS], AX.X, ALU.max)
                    dve.drain()
                    nc.vector.tensor_tensor(heads(row_top, a), heads(row_top, a), tile_top[:, 0:HEADS], ALU.max)
                    dve.drain()
            nc.vector.scalar_tensor_tensor(once[:], twins[:], 0.0, valid[:], ALU.is_equal, ALU.mult)
            nc.vector.scalar_tensor_tensor(rep[:], elders[:], 0.0, valid[:], ALU.is_equal, ALU.mult)
            nc.vector.tensor_tensor(p_edge[:, :, 0:HEADS], att[:], row_top[:], ALU.subtract)
            nc.vector.tensor_scalar(p_zero[:], row_top[:], -1.0, None, ALU.mult)
            nc.vector.tensor_scalar(p_diag[:], row_top[:], -1.0, DIAG_SCORE, ALU.mult, ALU.add).then_inc(exp_in, 1)
            dve.drain()
            nc.vector.scalar_tensor_tensor(out_slot_f[:], src[:], -NONE, rep[:], ALU.add, ALU.mult)
            dve.drain()
            nc.vector.tensor_scalar(out_slot[:], out_slot_f[:], NONE, None, ALU.add)
            dve.wait_ge(exp_made, 1)
            nc.vector.tensor_copy(p_edge[:, :, HEADS], once[:])
            nc.vector.tensor_tensor(p_edge[:, :, 0:HEADS], p_edge[:, :, 0:HEADS],
                                    once[:].unsqueeze(2).to_broadcast([P, ET, HEADS]), ALU.mult)
            dve.drain()
            with dve.Fori(0, tiles) as b:
                nc.vector.tensor_copy(field[:, 0:HEADS + 1], heads(p_edge, b))
                nc.vector.tensor_copy(field[:, HEADS + 1:HEADS + 2], one(src, b))
                dve.drain()
                nc.vector.tensor_copy(field_out[:], field[:]).then_inc(sums_field, 1)
                dve.wait_ge(sums_spread, b + 1)
                nc.vector.tensor_copy(spread_sb[:, 0:2 * P], ps_b[:, 0:2 * P])
                dve.drain()
                with dve.Fori(0, tiles) as a:
                    nc.vector.tensor_scalar(same, spread_sb[:, P:2 * P], one(src, a), None, ALU.is_equal)
                    dve.drain()
                    for i in range(2):
                        nc.vector.tensor_tensor(pair_att[:, 4 * i:4 * i + 4], ps_a[:, i].rearrange("p (h e) -> p h e", e=P),
                                                same.unsqueeze(1).to_broadcast([P, 4, P]), ALU.mult)
                    nc.vector.tensor_tensor(pair_att[:, HEADS], spread_sb[:, 0:P], same, ALU.mult)
                    dve.drain()
                    nc.vector.tensor_reduce(tile_top[:], pair_att, AX.X, ALU.add)
                    dve.drain()
                    nc.vector.tensor_tensor(heads(row_sum, a), heads(row_sum, a), tile_top[:], ALU.add)
                    dve.drain()

        def edge_weights(dve, tiles):
            def one(t, a):
                return t[:, bass.ds(a, 1)]

            def heads(t, a):
                return t[:, bass.ds(a, 1)].rearrange("p o h -> p (o h)")

            with dve.Fori(0, tiles) as a:
                dve.wait_ge(nd_in, 16 * a + 16)
                nc.vector.tensor_copy(head_tmp[:, 0], heads(p_zero, a))
                nc.vector.tensor_copy(head_tmp[:, 1], heads(p_diag, a))
                nc.vector.tensor_copy(head_tmp9[:], heads(p_edge, a))
                nc.vector.tensor_copy(tile_top[:], heads(row_sum, a))
                dve.drain()
                nc.vector.tensor_tensor(n_free[:], nd[:, 0:1], tile_top[:, HEADS:HEADS + 1], ALU.subtract)
                nc.vector.tensor_tensor(head_tmp[:, 2], head_tmp[:, 1], tile_top[:, 0:HEADS], ALU.add)
                dve.drain()
                nc.vector.scalar_tensor_tensor(z_head[:], head_tmp[:, 0], n_free[:], head_tmp[:, 2], ALU.mult, ALU.add)
                dve.drain()
                nc.vector.reciprocal(iz_head[:], z_head[:])
                dve.drain()
                mean = 1.0 / HEADS
                nc.vector.scalar_tensor_tensor(z_head[:], head_tmp[:, 0], mean, iz_head[:], ALU.mult, ALU.mult,
                                               accum_out=w_tmp[:, 0:1])
                nc.vector.scalar_tensor_tensor(head_tmp[:, 2], head_tmp[:, 1], mean, iz_head[:], ALU.mult, ALU.mult,
                                               accum_out=w_tmp[:, 1:2])
                nc.vector.scalar_tensor_tensor(tile_top[:, 0:HEADS], head_tmp9[:, 0:HEADS], mean, iz_head[:], ALU.mult, ALU.mult,
                                               accum_out=w_edge[:, 0:1])
                dve.drain()
                nc.vector.tensor_copy(one(w_zero, a), w_tmp[:, 0:1])
                nc.vector.tensor_tensor(w_edge[:, 1:2], w_tmp[:, 0:1], head_tmp9[:, HEADS:HEADS + 1], ALU.mult)
                nc.vector.tensor_tensor(w_tmp[:, 0:1], w_tmp[:, 0:1], nd[:, 1:2], ALU.mult)
                dve.drain()
                nc.vector.tensor_tensor(one(w_diff, a), w_edge[:, 0:1], w_edge[:, 1:2], ALU.subtract)
                nc.vector.scalar_tensor_tensor(one(w_own, a), w_tmp[:, 1:2], 1.0, w_tmp[:, 0:1], ALU.add,
                                               ALU.subtract).then_inc(nd_used, 1)
            dve.drain()
            nc.vector.memset(fix_sum, 0.0).then_inc(weighed, 1)
            dve.drain()

        def edge_rows(dve, tiles):
            def one(t, a):
                return t[:, bass.ds(a, 1)]

            with dve.Fori(0, tiles) as a:
                nc.vector.tensor_copy(field_out[:, 0:1], one(src, a)).then_inc(src_field, 1)
                nc.vector.memset(fix_sum, 0.0)
                dve.wait_ge(src_spread, a + 1)
                nc.vector.tensor_copy(spread_sb[:, 0:P], ps_b[:, 0:P])
                dve.drain()
                with dve.Fori(0, tiles) as b:
                    n = a * tiles + b
                    nc.vector.tensor_scalar(same, spread_sb[:, 0:P], one(src, b), None, ALU.is_equal)
                    dve.wait_ge(obj_in, 16 * n + 16)
                    nc.vector.tensor_scalar(fix, x_obj, one(w_diff, b), None, ALU.mult).then_inc(pair_room, 1)
                    dve.drain()
                    nc.vector.tensor_copy(pair_out, same).then_inc(pair_ready, 1)
                    dve.wait_ge(pair_done, n + 1)
                    nc.vector.tensor_tensor(fix_sum, fix_sum, ps_a[:, 0], ALU.add)
                    dve.drain()
                dve.wait_ge(own_in, 16 * a + 16)
                nc.vector.scalar_tensor_tensor(fix_part, x_src, one(w_own, a), fix_sum, ALU.mult, ALU.add)
                dve.drain()
                dve.wait_ge(g_src_in, 16 * a + 16)
                nc.vector.scalar_tensor_tensor(fix_y, g_src, one(w_zero, a), fix_part, ALU.mult, ALU.add)
                dve.drain()
                nc.vector.bn_stats(fix_stats[:], fix_y)
                dve.drain()
                nc.vector.tensor_tensor(fix_small[:, 0:1], fix_stats[:, 1:2], fix_stats[:, 4:5], ALU.add)
                nc.vector.tensor_tensor(fix_small[:, 1:2], fix_stats[:, 1:2], fix_stats[:, 4:5], ALU.subtract)
                nc.vector.tensor_tensor(fix_small[:, 2:3], fix_stats[:, 2:3], fix_stats[:, 5:6], ALU.add)
                dve.drain()
                nc.vector.scalar_tensor_tensor(fix_small[:, 3:4], fix_small[:, 1:2], H / 4.0, fix_small[:, 1:2],
                                               ALU.mult, ALU.mult)
                dve.drain()
                nc.vector.tensor_tensor(fix_small[:, 4:5], fix_small[:, 2:3], fix_small[:, 3:4], ALU.add).then_inc(fix_var, 1)
                dve.wait_ge(fix_std, a + 1)
                nc.vector.reciprocal(fix_small[:, 6:7], fix_small[:, 5:6])
                dve.drain()
                nc.vector.scalar_tensor_tensor(fix_small[:, 7:8], fix_small[:, 0:1], -0.5, fix_small[:, 6:7],
                                               ALU.mult, ALU.mult)
                dve.drain()
                nc.vector.tensor_scalar(fix_out, fix_y, fix_small[:, 6:7], fix_small[:, 7:8], ALU.mult,
                                        ALU.add).then_inc(fixed, 1)

        @block.vector
        def _(dve):
            edge_index(dve)
            for c in range(CH):
                scale_x(dve, c)
                select_chunk(dve, 0, c, True)
            dve.wait_ge(diag_in, 16)
            nc.vector.tensor_scalar(diag[:], diag_raw[:], 1.0, None, ALU.is_equal).then_inc(diag_made, 1)
            dve.wait_ge(diag_made, 1)

            def group(g):
                for c in range(CH):
                    select_chunk(dve, g, c, False)
                    if c == 1:
                        coefficients(dve, g - 1)
                    if c == 3:
                        mix_rows(dve, g - 1)
                    if c == 4:
                        scale_rows(dve, g - 1)

            group(1)
            with dve.Fori(2, SLOT_GROUP + 1) as g:
                group(g)
            edge_slots(dve)
            with dve.Fori(SLOT_GROUP + 1, SCORE_GROUP + 1) as g:
                group(g)
            tiles = dve.value_load(n_tiles[0:1, 0:1], min_val=1, max_val=ET)
            edge_scores(dve, tiles)
            with dve.Fori(SCORE_GROUP + 1, GR) as g:
                group(g)
            coefficients(dve, GR - 1)
            mix_rows(dve, GR - 1)
            scale_rows(dve, GR - 1)
            edge_weights(dve, tiles)
            edge_rows(dve, tiles)

        @block.scalar
        def _(act):
            for c in range(CH):
                act.wait_ge(scale_made, 2 * (c + 1))
                if c >= 2:
                    act.wait_ge(lo_made, c - 1)
                for t in range(TC):
                    n = TC * c + t
                    nc.scalar.activation(x_scaled[:, c % 2, t], x_raw[:, c % 2, t], ACT.Copy,
                                         scale=up[:, n:n + 1]).then_inc(scaled_x, 1)
                    act.wait_ge(scaled_x, n + 1)
                    nc.scalar.activation(x_hi[:, n], x_scaled[:, c % 2, t], ACT.Copy).then_inc(hi_made, 1)

            def finish_group(act, g, first):
                for k in range(KB):
                    act.wait_ge(bank_done, KB * g + k + 1)
                    if not first and k == 0:
                        act.wait_ge(g_sent, 16 * g)
                        act.wait_ge(y_made, KB * g)
                    nc.scalar.activation(g_row[:, k], ps_g[k][:], ACT.Copy).then_inc(bank_read, 1)
                act.wait_ge(coef_made, g + 1)
                act.dma_start(nd_rows[g], nd_row[:]).then_inc(nd_sent, 16)
                act.wait_ge(bank_read, KB * (g + 1))
                act.dma_start(g_rows[g], g_row[:]).then_inc(g_sent, 16)
                act.wait_ge(xrow_in, 16 * (g + 1))
                for k in range(KB):
                    nc.scalar.activation(x_row[:, k], x_row[:, k], ACT.Copy,
                                         scale=w_self[:, k:k + 1]).then_inc(xpart_made, 1)
                act.wait_ge(mv_made, g + 1)
                if first:
                    act.wait_ge(consts, 2)
                nc.scalar.activation(std[:], sq_sum[:], ACT.Sqrt, bias=eps_col[:], scale=1.0 / H).then_inc(std_made, 1)
                act.wait_ge(shift_made, g + 1)
                for k in range(KB):
                    nc.scalar.activation(y_row[:, k], y_row[:, k], ACT.Identity, bias=shift[:, k:k + 1],
                                         scale=rstd[:, k:k + 1]).then_inc(out_made, 1)
                act.wait_ge(out_made, KB * (g + 1))
                act.dma_start(out_rows[g], y_row[:]).then_inc(out_sent, 16)

            finish_group(act, 0, True)
            with act.Fori(1, SCORE_GROUP) as g:
                finish_group(act, g, False)
            act.wait_ge(slots_made, 1)
            tiles = act.value_load(n_tiles[0:1, 0:1], min_val=1, max_val=ET)
            with act.Fori(0, tiles) as a:
                act.wait_ge(ends_turned, 2 * a + 1)
                nc.scalar.activation(x_src_t, ps_a[:, 0].rearrange("p (c e) -> p c e", e=P), ACT.Copy).then_inc(turned_read, 1)
                act.wait_ge(ends_turned, 2 * a + 2)
                nc.scalar.activation(x_obj_t, ps_a[:, 1].rearrange("p (c e) -> p c e", e=P), ACT.Copy).then_inc(turned_read, 1)
            act.wait_ge(exp_in, 1)
            nc.scalar.activation(p_edge[:, :, 0:HEADS], p_edge[:, :, 0:HEADS], ACT.Exp)
            nc.scalar.activation(p_zero[:], p_zero[:], ACT.Exp)
            nc.scalar.activation(p_diag[:], p_diag[:], ACT.Exp).then_inc(exp_made, 1)
            with act.Fori(SCORE_GROUP, GR) as g:
                finish_group(act, g, False)
            with act.Fori(0, tiles) as a:
                act.wait_ge(fix_var, a + 1)
                nc.scalar.activation(fix_small[:, 5:6], fix_small[:, 4:5], ACT.Sqrt, bias=eps_col[:],
                                     scale=1.0 / H).then_inc(fix_std, 1)

        @block.tensor
        def _(pe):
            def multiply_group(pe, g, first, between=None):
                for c in range(CH):
                    pe.wait_ge(sel_made, g * CH + c + 1)
                    if first:
                        pe.wait_ge(hi_made, TC * (c + 1))
                        pe.wait_ge(lo_made, c + 1)
                    if c == CH - 1:
                        pe.wait_ge(chunk_counted, g * CH + CH)
                        if first:
                            pe.wait_ge(consts, 1)
                        else:
                            pe.wait_ge(coef_made, g)
                        for k in range(KB):
                            for t in range(TC):
                                last = nc.tensor.matmul(ps_cnt[:, k:k + 1], count[:, t, k * P:(k + 1) * P], ones[:],
                                                        start=(t == 0), stop=(t == TC - 1))
                        last.then_inc(counted, 1)
                    for k in range(KB):
                        if c == 0 and not first:
                            pe.wait_ge(bank_read, KB * (g - 1) + k + 1)
                        for t in range(TC):
                            w = sel[:, c % SEL_BUFS, t, k * P:(k + 1) * P]
                            n = TC * c + t
                            nc.tensor.matmul(ps_g[k][:], w, x_hi[:, n], start=(n == 0), stop=False)
                            last = nc.tensor.matmul(ps_g[k][:], w, x_lo[:, n], start=False, stop=(n == NT - 1))
                        if c == CH - 1:
                            last.then_inc(bank_done, 1)
                    if c < CH - 1:
                        last.then_inc(sel_used, 1)
                    if c == CH // 2 and between:
                        between()

            def edge_bases():
                pe.wait_ge(tables_made, 5)
                pe.wait_ge(total_made, 1)
                nc.tensor.matmul(ps_b[:, 0:1], before[:], live_total[:], start=True, stop=True)
                nc.tensor.matmul(ps_b[:, 1:2], all_ones[:], live_total[:], start=True, stop=True).then_inc(base_made, 1)

            def spread_field(column, dst):
                return nc.tensor.matmul(dst, field_out[:, column:column + 1].to_broadcast([P, P]), ident[:],
                                        start=True, stop=True)

            def edge_products():
                pe.wait_ge(weights_in, 64)
                with pe.Fori(0, tiles) as a:
                    pe.wait_ge(ends_in, 32 * a + 32)
                    for i, ends in enumerate((x_src, x_obj)):
                        for c in range(HC):
                            last = nc.tensor.transpose(ps_a[:, i, c * P:(c + 1) * P], ends[:, c * P:(c + 1) * P], ident[:])
                        last.then_inc(ends_turned, 1)
                    for i, (turned, w) in enumerate(((x_src_t, wq_sb), (x_obj_t, wk_sb))):
                        pe.wait_ge(turned_read, 2 * a + i + 1)
                        for c in range(HC):
                            last = nc.tensor.matmul(ps_a[:, i], turned[:, c], w[:, c], start=(c == 0), stop=(c == HC - 1))
                        last.then_inc(qk_made, 1)
                with pe.Fori(0, tiles) as b:
                    pe.wait_ge(fields_made, b + 1)
                    for h in range(HEADS):
                        spread_field(h, ps_a[:, h // 4, (h % 4) * P:(h % 4 + 1) * P])
                    for i in range(3):
                        last = spread_field(HEADS + i, ps_b[:, i * P:(i + 1) * P])
                    last.then_inc(spread, 1)
                with pe.Fori(0, tiles) as b:
                    pe.wait_ge(sums_field, b + 1)
                    for h in range(HEADS):
                        spread_field(h, ps_a[:, h // 4, (h % 4) * P:(h % 4 + 1) * P])
                    for i in range(2):
                        last = spread_field(HEADS + i, ps_b[:, i * P:(i + 1) * P])
                    last.then_inc(sums_spread, 1)

            multiply_group(pe, 0, True)
            with pe.Fori(1, SLOT_GROUP) as g:
                multiply_group(pe, g, False)
            multiply_group(pe, SLOT_GROUP, False, edge_bases)
            with pe.Fori(SLOT_GROUP + 1, SCORE_GROUP) as g:
                multiply_group(pe, g, False)
            pe.wait_ge(slots_made, 1)
            tiles = pe.value_load(n_tiles[0:1, 0:1], min_val=1, max_val=ET)
            multiply_group(pe, SCORE_GROUP, False, edge_products)
            with pe.Fori(SCORE_GROUP + 1, GR) as g:
                multiply_group(pe, g, False)
            with pe.Fori(0, tiles) as a:
                pe.wait_ge(src_field, a + 1)
                spread_field(0, ps_b[:, 0:P]).then_inc(src_spread, 1)
                with pe.Fori(0, tiles) as b:
                    pe.wait_ge(pair_ready, a * tiles + b + 1)
                    nc.tensor.matmul(ps_a[:, 0], pair_out, fix, start=True, stop=True).then_inc(pair_done, 1)


def kernel(x, adj, L0_gnn_rel_pair_index, L0_gnn_Wq, L0_gnn_bq, L0_gnn_Wk, L0_gnn_bk):
    import concourse.bacc as bacc
    from concourse.bass_utils import run_bass_kernel_spmd

    x, adj = np.asarray(x), np.asarray(adj)
    N, H = x.shape
    GC = KB * P
    adj_t = np.ascontiguousarray(adj.reshape(N // GC, GC, N // P, P).transpose(0, 3, 2, 1))
    adj_diag = np.ascontiguousarray(np.diagonal(adj).reshape(N // P, P).T)
    pairs = np.asarray(L0_gnn_rel_pair_index)
    arrays = {"x": x, "adj_t": adj_t, "adj_diag": adj_diag, "pairs": pairs,
              "wq_t": np.ascontiguousarray(np.asarray(L0_gnn_Wq).T), "bq": np.asarray(L0_gnn_bq),
              "wk_t": np.ascontiguousarray(np.asarray(L0_gnn_Wk).T), "bk": np.asarray(L0_gnn_bk)}
    nc = bacc.Bacc("TRN2", target_bir_lowering=False, num_devices=1)
    args = {n: nc.dram_tensor(n, a.shape, mybir.dt.from_np(a.dtype), kind="ExternalInput").ap() for n, a in arrays.items()}
    out = nc.dram_tensor("out", (N, H), F32, kind="ExternalOutput").ap()
    scratch = {"g_table": ((N, H), F32), "nd_table": ((N, 2), F32),
               "edge_list": ((P * edge_columns(pairs.shape[0]), 2), mybir.dt.int32)}
    scratch = {n: nc.dram_tensor(n, s, t, kind="Internal").ap() for n, (s, t) in scratch.items()}
    build(nc, *args.values(), out, *scratch.values())
    r = run_bass_kernel_spmd(nc, [arrays], core_ids=[0])
    return r.results[0]["out"]
```

```python
from contextlib import ExitStack

import numpy as np
import concourse.bass as bass
from concourse import mybir

ALU = mybir.AluOpType
ACT = mybir.ActivationFunctionType
AX = mybir.AxisListType
F32 = mybir.dt.float32
BF16 = mybir.dt.bfloat16
F16 = mybir.dt.float16
I32 = mybir.dt.int32

P = 128
KB = 4
TC = 4
RAW_BUFS = 4
SLOT_GROUP = 3
SCORE_GROUP = 5
SEL_BUFS = 4
HEADS = 8
STAGE = 16
LN_EPS = 1e-5
DIAG_SCORE = 1e-7
NONE = float(2 ** 20)
LOWEST = -1e38
E_OFF = float(np.exp(np.float32(-DIAG_SCORE)))


def edge_columns(E):
    n = -(-E // P)
    while E % n:
        n += 1
    return n


def build(nc, x, adj_t, adj_diag, pairs, wq_t, bq, wk_t, bk, out, g_table, nd_table, part_table):
    N, H = x.shape
    E = pairs.shape[0]
    ET = edge_columns(E)
    EP = E // ET
    DK = H // HEADS
    assert ET % STAGE == 0
    HC = H // P
    NT = N // P
    GR = N // (P * KB)
    GC = KB * P
    CH = NT // TC

    with ExitStack() as ctx:
        def sb(name, shape, dt):
            return ctx.enter_context(nc.sbuf_tensor(name, shape, dt))

        def psum(name, shape, dt):
            return ctx.enter_context(nc.psum_tensor(name, shape, dt))

        def sem(name):
            return ctx.enter_context(nc.semaphore(name))

        x_space = sb("x_space", [P, 4, TC, H], F32)
        x_raw, x_scaled = x_space[:, 0:2], x_space[:, 2:4]
        x_hi = sb("x_hi", [P, NT, H], F16)
        x_lo = sb("x_lo", [P, NT, H], F16)
        row_max = sb("row_max", [P, NT], F32)
        expo = sb("expo", [P, NT], I32)
        expo_dn = sb("expo_dn", [P, NT], I32)
        up = sb("up", [P, NT], F32)
        down = sb("down", [P, NT], F32)
        adj_raw = sb("adj_raw", [P, RAW_BUFS, TC, GC], F32)
        sel = sb("sel", [P, SEL_BUFS, TC, GC], BF16)
        count = sb("count", [P, TC, GC], BF16)
        ones = sb("ones", [P, 1], BF16)
        diag_raw = sb("diag_raw", [P, NT], F32)
        diag = sb("diag", [P, NT], F32)
        z_row = sb("z_row", [P, KB], F32)
        inv_z = sb("inv_z", [P, KB], F32)
        w_off = sb("w_off", [P, KB], F32)
        w_d = sb("w_d", [P, KB], F32)
        w_self = sb("w_self", [P, KB], F32)
        x_row = sb("x_row", [P, KB, H], F32)
        g_row = sb("g_row", [P, KB, H], F32)
        nd_row = sb("nd_row", [P, KB, 2], F32)
        y_row = sb("y_row", [P, KB, H], F32)
        stats = sb("stats", [P, KB, 6], F32)
        mean = sb("mean", [P, KB], F32)
        gap = sb("gap", [P, KB], F32)
        gap_sq = sb("gap_sq", [P, KB], F32)
        var = sb("var", [P, KB], F32)
        sq_sum = sb("sq_sum", [P, KB], F32)
        std = sb("std", [P, KB], F32)
        rstd = sb("rstd", [P, KB], F32)
        shift = sb("shift", [P, KB], F32)
        eps_col = sb("eps_col", [P, 1], F32)

        pair_sb = sb("pair_sb", [EP, ET, 2], I32)
        adj_index = sb("adj_index", [EP, ET], I32)
        index_part = sb("index_part", [EP, 3, ET], I32)
        digits_i = sb("digits_i", [EP, ET, 4], I32)
        digits = sb("digits", [EP, ET, 4], BF16)
        lane_i = sb("lane_i", [EP, P], I32)
        lane = sb("lane", [EP, P], BF16)
        end_digits = sb("end_digits", [P, 4], F32)
        p_field = sb("p_field", [P, HEADS + 1], F32)
        adj_val = sb("adj_val", [EP, ET], F32)
        off_diag = sb("off_diag", [EP, ET], F32)
        live = sb("live", [EP, ET], F32)
        unit = sb("unit", [EP, ET], F32)
        live_sum = sb("live_sum", [EP, ET], F32)
        live_total = sb("live_total", [EP, 1], BF16)
        before = sb("before", [EP, P], BF16)
        all_ones = sb("all_ones", [EP, P], BF16)
        base_total = sb("base_total", [P, 2], F32)
        place = sb("place", [EP, ET], F32)
        slot_f = sb("slot_f", [EP, ET], F32)
        slot_16 = sb("slot_16", [EP, ET], BF16)
        n_i = sb("n_i", [P, 1], I32)
        n_tiles = sb("n_tiles", [P, 1], I32)
        edge_sb = sb("edge_sb", [P, ET, 2], I32)
        seq_i = sb("seq_i", [P, ET], I32)
        seq = sb("seq", [P, ET], F32)
        valid = sb("valid", [P, ET], F32)
        src = sb("src", [P, ET], F32)
        key = sb("key", [P, ET], F32)
        att = sb("att", [P, ET, HEADS], F32)
        row_top = sb("row_top", [P, ET, HEADS], F32)
        twins = sb("twins", [P, ET], F32)
        elders = sb("elders", [P, ET], F32)
        once = sb("once", [P, ET], F32)
        rep = sb("rep", [P, ET], F32)
        p_edge = sb("p_edge", [P, ET, HEADS + 1], F32)
        p_zero = sb("p_zero", [P, ET, HEADS], F32)
        p_diag = sb("p_diag", [P, ET, HEADS], F32)
        row_sum = sb("row_sum", [P, ET, HEADS + 1], F32)
        w_diff = sb("w_diff", [P, ET], F32)
        w_zero = sb("w_zero", [P, ET], F32)
        w_own = sb("w_own", [P, ET], F32)
        out_slot_f = sb("out_slot_f", [P, ET], F32)
        out_slot = sb("out_slot", [P, ET], I32)
        ident = sb("ident", [P, P], F32)
        bq_sb = sb("bq_sb", [P, H], F32)
        bk_sb = sb("bk_sb", [P, H], F32)
        field = sb("field", [P, HEADS + 3], F32)
        field_out = sb("field_out", [P, HEADS + 3], F32)
        head_tmp9 = sb("head_tmp9", [P, HEADS + 1], F32)
        adj_stage = sb("adj_stage", [EP, STAGE], F32)
        pair_mark = sb("pair_mark", [P, 1], F32)
        stage = sb("stage", [EP, STAGE], I32)
        ends = sb("ends", [P, 2], I32)
        obj_ends = sb("obj_ends", [P, 2], I32)
        row_index = sb("row_index", [P, 1], I32)
        tile_top = sb("tile_top", [P, HEADS + 1], F32)
        tile_cnt = sb("tile_cnt", [P, 2], F32)
        nd = sb("nd", [P, 2], F32)
        n_free = sb("n_free", [P, 1], F32)
        z_head = sb("z_head", [P, HEADS], F32)
        iz_head = sb("iz_head", [P, HEADS], F32)
        head_tmp = sb("head_tmp", [P, 3, HEADS], F32)
        w_edge = sb("w_edge", [P, 2], F32)
        w_tmp = sb("w_tmp", [P, 2], F32)
        fix_stats = sb("fix_stats", [P, 6], F32)
        fix_small = sb("fix_small", [P, 8], F32)

        wq_sb, wk_sb = x_scaled[:, 0], x_scaled[:, 1]
        x_src, x_obj = x_raw[:, 0, 0], x_raw[:, 0, 1]
        x_src_t = x_raw[:, 0, 2].rearrange("p (c e) -> p c e", e=P)
        x_obj_t = x_raw[:, 0, 3].rearrange("p (c e) -> p c e", e=P)
        q_sb, k_sb = x_raw[:, 1, 0], x_raw[:, 1, 1]
        fix, fix_sum = x_raw[:, 1, 2], x_raw[:, 1, 3]
        fix_part, fix_y = q_sb, k_sb
        chosen = x_space[:].rearrange("p b t h -> p (b t h)")[0:EP, 0:ET * P // 2].bitcast(BF16).rearrange("p (c j) -> p c j", j=P)
        pair_space = x_scaled[:, 0].rearrange("p t h -> p (t h)")
        pair_att = pair_space[:, 0:(HEADS + 1) * P].rearrange("p (h e) -> p h e", e=P)
        spread_sb = pair_space[:, (HEADS + 1) * P:(HEADS + 4) * P]
        same, younger, apart, pair_out = (pair_space[:, (HEADS + i) * P:(HEADS + i + 1) * P] for i in (4, 5, 6, 7))
        g_src, fix_out = x_scaled[:, 1, 0], x_scaled[:, 1, 1]
        assert HC == TC and H == HC * P

        ps_a = psum("ps_a", [P, 2, H], F32)
        ps_b = psum("ps_b", [P, H], F32)
        ps_g = [psum(f"ps_g{k}", [P, H], F32) for k in range(KB)]
        ps_cnt = psum("ps_cnt", [P, H], F32)

        adj_in = [sem(f"adj_in{b}") for b in range(RAW_BUFS)]
        x_in = [sem(f"x_in{b}") for b in range(2)]
        x_first = [sem(f"x_first{t}") for t in range(TC)]
        diag_in = sem("diag_in")
        sel_made = sem("sel_made")
        chunk_counted = sem("chunk_counted")
        sel_used = sem("sel_used")
        scale_made = sem("scale_made")
        hi_made = sem("hi_made")
        lo_made = sem("lo_made")
        consts = sem("consts")
        x_step = sem("x_step")
        coef_step = sem("coef_step")
        join_step = sem("join_step")
        rstd_made = sem("rstd_made")
        diag_made = sem("diag_made")
        counted = sem("counted")
        coef_made = sem("coef_made")
        bank_done = sem("bank_done")
        bank_read = sem("bank_read")
        xrow_in = sem("xrow_in")
        xpart_made = sem("xpart_made")
        y_made = sem("y_made")
        stats_made = sem("stats_made")
        mv_made = sem("mv_made")
        std_made = sem("std_made")
        unscale_made = sem("unscale_made")
        shift_made = sem("shift_made")
        out_made = sem("out_made")
        out_sent = sem("out_sent")
        g_sent = sem("g_sent")

        pairs_in = sem("pairs_in")
        weights_in = sem("weights_in")
        index_made = sem("index_made")
        adj_val_in = sem("adj_val_in")
        tables_made = sem("tables_made")
        cleared = sem("cleared")
        total_made = sem("total_made")
        base_made = sem("base_made")
        slots_made = sem("slots_made")
        listed = sem("listed")
        chosen_made = sem("chosen_made")
        digits_out = sem("digits_out")
        row_field = sem("row_field")
        row_spread = sem("row_spread")
        sum_ready = sem("sum_ready")
        sum_done = sem("sum_done")
        ends_in = sem("ends_in")
        ends_turned = sem("ends_turned")
        turned_read = sem("turned_read")
        qk_made = sem("qk_made")
        qk_read = sem("qk_read")
        att_made = sem("att_made")
        fields_made = sem("fields_made")
        spread = sem("spread")
        exp_in = sem("exp_in")
        exp_made = sem("exp_made")
        sums_field = sem("sums_field")
        sums_spread = sem("sums_spread")
        nd_sent = sem("nd_sent")
        nd_in = sem("nd_in")
        nd_used = sem("nd_used")
        src_field = sem("src_field")
        src_spread = sem("src_spread")
        own_in = sem("own_in")
        g_src_in = sem("g_src_in")
        obj_in = sem("obj_in")
        pair_ready = sem("pair_ready")
        pair_done = sem("pair_done")
        pair_added = sem("pair_added")
        fix_var = sem("fix_var")
        fix_std = sem("fix_std")
        fixed = sem("fixed")
        weighed = sem("weighed")
        pair_room = sem("pair_room")
        fix_sent = sem("fix_sent")
        staged = sem("staged")
        stage_ready = sem("stage_ready")
        parts_done = sem("parts_done")
        part_sent = sem("part_sent")
        part_in = sem("part_in")

        x_tiles = x.rearrange("(c t p) h -> c p t h", p=P, t=TC)
        adj_chunks = adj_t.rearrange("g p (c t) i -> g c p t i", t=TC)
        x_rows = x.rearrange("(g k p) h -> g p k h", p=P, k=KB)
        out_rows = out.rearrange("(g k p) h -> g p k h", p=P, k=KB)
        nd_rows = nd_table.rearrange("(g k p) c -> g p k c", p=P, k=KB)
        adj_flat = adj_t.rearrange("g p t (i o) -> (g p t i) o", o=1)
        g_rows = g_table.rearrange("(g k p) h -> g p k h", p=P, k=KB)

        assert SCORE_GROUP + 2 == GR - 1 and SLOT_GROUP + 2 == SCORE_GROUP
        block = ctx.enter_context(nc.Block())

        @block.sync
        def _(sp):
            def load_adj(g, c, wait):
                b = c % RAW_BUFS
                if wait:
                    sp.wait_ge(chunk_counted, g * CH + c + 1 - RAW_BUFS)
                sp.dma_start(adj_raw[:, b], adj_chunks[g, c]).then_inc(adj_in[b], 16)

            for c in range(CH):
                if c >= 2:
                    sp.wait_ge(hi_made, TC * (c - 1))
                if c == 0:
                    for t in range(TC):
                        sp.dma_start(x_raw[:, 0, t], x_tiles[0, :, t]).then_inc(x_first[t], 16)
                else:
                    sp.dma_start(x_raw[:, c % 2], x_tiles[c]).then_inc(x_in[c % 2], 16)
                load_adj(0, c, c >= RAW_BUFS)
                if c == 0:
                    sp.dma_start(pair_sb[:], pairs.rearrange("(p t) c -> p t c", t=ET)).then_inc(pairs_in, 16)
                    sp.dma_start(diag_raw[:], adj_diag).then_inc(diag_in, 16)
            sp.dma_start(x_row[:], x_rows[0]).then_inc(xrow_in, 16)
            with sp.Fori(1, GR) as g:
                for c in range(CH):
                    load_adj(g, c, True)
                    if c == CH - 2:
                        sp.wait_ge(y_made, KB * g)
                        sp.dma_start(x_row[:], x_rows[g]).then_inc(xrow_in, 16)

        @block.gpsimd
        def _(pool):
            nc.gpsimd.memset(ones[:], 1.0).then_inc(consts, 1)
            nc.gpsimd.memset(eps_col[:], LN_EPS).then_inc(consts, 1)
            nc.gpsimd.memset(unit[:], 1.0).then_inc(tables_made, 1)
            nc.gpsimd.memset(all_ones[:], 1.0).then_inc(tables_made, 1)
            nc.gpsimd.memset(before[:], 1.0).then_inc(cleared, 1)
            nc.gpsimd.memset(ident[:], 0.0).then_inc(cleared, 1)
            pool.wait_ge(cleared, 2)
            nc.gpsimd.affine_select(out=before[:], in_=before[:], compare_op=ALU.is_gt, fill=0.0, base=0,
                                    pattern=[[1, P]], channel_multiplier=-1).then_inc(tables_made, 1)
            nc.gpsimd.affine_select(out=ident[:], in_=ident[:], compare_op=ALU.not_equal, fill=1.0, base=0,
                                    pattern=[[1, P]], channel_multiplier=-1).then_inc(tables_made, 1)
            nc.gpsimd.iota(seq_i[:], pattern=[[P, ET]], base=0, channel_multiplier=1).then_inc(tables_made, 1)
            nc.gpsimd.iota(lane_i[:], pattern=[[1, P]], base=0, channel_multiplier=0).then_inc(tables_made, 1)
            def split_low(pool, n, count):
                pool.wait_ge(hi_made, n + count)
                c, t = n // TC, n % TC
                nc.gpsimd.tensor_tensor(x_lo[:, n:n + count], x_scaled[:, c % 2, t:t + count], x_hi[:, n:n + count],
                                        ALU.subtract).then_inc(lo_made, count)

            def adj_of_edges(pool, c):
                pool.indirect_dma_start(
                    out=adj_stage[:, c:c + 1], out_offset=None, in_=adj_flat,
                    in_offset=bass.IndirectOffsetOnAxis(ap=stage[:, c:c + 1], axis=0)).then_inc(adj_val_in, 16)

            for t in range(TC):
                split_low(pool, t, 1)
            per_chunk = STAGE // (CH - 1)
            for c in range(1, CH):
                for t in range(TC):
                    split_low(pool, TC * c + t, 1)
                if c == 1:
                    pool.wait_ge(index_made, 1)
                    nc.gpsimd.tensor_copy(stage[:], adj_index[:, 0:STAGE]).then_inc(stage_ready, 1)
                pool.wait_ge(stage_ready, 1)
                for i in range(per_chunk * (c - 1), per_chunk * c if c < CH - 1 else STAGE):
                    adj_of_edges(pool, i)
            pool.wait_ge(adj_val_in, 16 * STAGE)
            nc.gpsimd.tensor_copy(adj_val[:, 0:STAGE], adj_stage[:]).then_inc(staged, 1)
            pool.sem_inc(att_made, 1)
            pool.sem_inc(nd_used, 1)
            pool.sem_inc(pair_room, 1)
            with pool.Fori(1, ET // STAGE) as r:
                nc.gpsimd.tensor_copy(stage[:], adj_index[:, bass.ds(r * STAGE, STAGE)])
                pool.drain()
                for c in range(STAGE):
                    adj_of_edges(pool, c)
                pool.wait_ge(adj_val_in, 16 * STAGE * r + 16 * STAGE)
                nc.gpsimd.tensor_copy(adj_val[:, bass.ds(r * STAGE, STAGE)], adj_stage[:]).then_inc(staged, 1)
            pool.wait_ge(listed, 1)
            tiles = pool.value_load(n_tiles[0:1, 0:1], min_val=1, max_val=ET)

            def gather(dst, table, end, ends=ends):
                return pool.indirect_dma_start(
                    out=dst, out_offset=None, in_=table,
                    in_offset=bass.IndirectOffsetOnAxis(ap=ends[:, end:end + 1], axis=0))

            with pool.Fori(0, tiles) as a:
                pool.wait_ge(att_made, a + 1)
                nc.gpsimd.tensor_copy(ends[:], edge_sb[:, bass.ds(a, 1)].rearrange("p o c -> p (o c)"))
                pool.drain()
                gather(x_src, x, 0).then_inc(ends_in, 16)
                gather(x_obj, x, 1).then_inc(ends_in, 16)
                pool.drain()
            pool.wait_ge(nd_sent, 16 * GR)
            with pool.Fori(0, tiles) as a:
                pool.wait_ge(nd_used, a + 1)
                nc.gpsimd.tensor_copy(ends[:], edge_sb[:, bass.ds(a, 1)].rearrange("p o c -> p (o c)"))
                pool.drain()
                gather(nd[:], nd_table, 0).then_inc(nd_in, 16)
                pool.drain()
            with pool.Fori(0, tiles) as a:
                nc.gpsimd.tensor_copy(ends[:], edge_sb[:, bass.ds(a, 1)].rearrange("p o c -> p (o c)"))
                pool.drain()
                gather(x_src, x, 0).then_inc(own_in, 16)
                with pool.Fori(0, tiles) as b:
                    n = a * tiles + b
                    pool.wait_ge(pair_room, n + 1)
                    nc.gpsimd.tensor_copy(obj_ends[:], edge_sb[:, bass.ds(b, 1)].rearrange("p o c -> p (o c)"))
                    pool.drain()
                    gather(x_obj, x, 1, obj_ends).then_inc(obj_in, 16)
                    pool.drain()
                pool.wait_ge(parts_done, a + 1)
                pool.dma_start(part_table[bass.ds(a, 1)].rearrange("o p h -> p (o h)"), fix_part).then_inc(part_sent, 16)
                pool.drain()
            with pool.Fori(0, tiles) as a:
                nc.gpsimd.tensor_copy(ends[:], edge_sb[:, bass.ds(a, 1)].rearrange("p o c -> p (o c)"))
                pool.drain()
                pool.dma_start(fix_sum, part_table[bass.ds(a, 1)].rearrange("o p h -> p (o h)")).then_inc(part_in, 16)
                pool.wait_ge(g_sent, 16 * (GR - 1 + KB))
                gather(g_src, g_table, 0).then_inc(g_src_in, 16)
                pool.wait_ge(fixed, a + 1)
                nc.gpsimd.tensor_copy(row_index[:], out_slot[:, bass.ds(a, 1)])
                pool.drain()
                pool.wait_ge(out_sent, 16 * (GR + 1))
                pool.indirect_dma_start(
                    out=out, out_offset=bass.IndirectOffsetOnAxis(ap=row_index[:], axis=0),
                    in_=fix_out, in_offset=None, bounds_check=N - 1, oob_is_err=False).then_inc(fix_sent, 16)
                pool.drain()
            pool.wait_ge(fix_sent, 16)

        def coefficients(dve, g):
            dve.wait_ge(counted, g + 1)
            if not (isinstance(g, int) and g == 0):
                dve.wait_ge(nd_sent, 16 * g)
                dve.wait_ge(xpart_made, KB * g)
            d = diag[:, bass.ds(g * KB, KB)]
            step = 5 * g
            nc.vector.tensor_copy(nd_row[:, :, 1], d)
            nc.vector.tensor_tensor(nd_row[:, :, 0], ps_cnt[:, 0:KB], d, ALU.subtract).then_inc(coef_step, 1)
            dve.wait_ge(coef_step, step + 1)
            nc.vector.tensor_scalar(z_row[:], nd_row[:, :, 0], E_OFF, 1.0, ALU.mult, ALU.add).then_inc(coef_step, 1)
            dve.wait_ge(coef_step, step + 2)
            nc.vector.reciprocal(inv_z[:], z_row[:]).then_inc(coef_step, 1)
            dve.wait_ge(coef_step, step + 3)
            nc.vector.tensor_scalar(w_off[:], inv_z[:], E_OFF, None, ALU.mult).then_inc(coef_step, 1)
            dve.wait_ge(coef_step, step + 4)
            nc.vector.tensor_tensor(w_d[:], w_off[:], d, ALU.mult).then_inc(coef_step, 1)
            dve.wait_ge(coef_step, step + 5)
            nc.vector.scalar_tensor_tensor(w_self[:], inv_z[:], 1.0, w_d[:], ALU.add,
                                           ALU.subtract).then_inc(coef_made, 1)

        def mix_rows(dve, g, k0=0, k1=KB, i=None):
            i = g if i is None else i
            ks = slice(k0, k1)
            for k in range(k0, k1):
                dve.wait_ge(bank_read, KB * g + k + 1)
                dve.wait_ge(xpart_made, KB * g + k + 1)
                if k == 0 and not (isinstance(g, int) and g == 0):
                    dve.wait_ge(out_sent, 16 * g)
                nc.vector.scalar_tensor_tensor(y_row[:, k], g_row[:, k], w_off[:, k:k + 1], x_row[:, k],
                                               ALU.mult, ALU.add).then_inc(y_made, 1)
                dve.wait_ge(y_made, KB * g + k + 1)
                nc.vector.bn_stats(stats[:, k], y_row[:, k]).then_inc(stats_made, 1)
            dve.wait_ge(stats_made, KB * g + k1)
            nc.vector.tensor_tensor(mean[:, ks], stats[:, ks, 1], stats[:, ks, 4], ALU.add).then_inc(join_step, 1)
            nc.vector.tensor_tensor(gap[:, ks], stats[:, ks, 1], stats[:, ks, 4], ALU.subtract).then_inc(join_step, 1)
            nc.vector.tensor_tensor(var[:, ks], stats[:, ks, 2], stats[:, ks, 5], ALU.add).then_inc(join_step, 1)
            dve.wait_ge(join_step, 4 * i + 2)
            nc.vector.scalar_tensor_tensor(gap_sq[:, ks], gap[:, ks], H / 4.0, gap[:, ks], ALU.mult,
                                           ALU.mult).then_inc(join_step, 1)
            dve.wait_ge(join_step, 4 * i + 4)
            nc.vector.tensor_tensor(sq_sum[:, ks], var[:, ks], gap_sq[:, ks], ALU.add).then_inc(mv_made, 1)

        def scale_rows(dve, g, k0=0, k1=KB, i=None):
            i = g if i is None else i
            ks = slice(k0, k1)
            dve.wait_ge(std_made, i + 1)
            nc.vector.reciprocal(rstd[:, ks], std[:, ks]).then_inc(rstd_made, 1)
            dve.wait_ge(rstd_made, i + 1)
            nc.vector.scalar_tensor_tensor(shift[:, ks], mean[:, ks], -0.5, rstd[:, ks], ALU.mult,
                                           ALU.mult).then_inc(shift_made, 1)

        def select_chunk(dve, g, c, first):
            b = c % RAW_BUFS
            dve.wait_ge(adj_in[b], (g * (CH // RAW_BUFS) + c // RAW_BUFS + 1) * 16)
            if c >= SEL_BUFS:
                dve.wait_ge(sel_used, g * (CH - 1) + c + 1 - SEL_BUFS)
            elif not first and c == SEL_BUFS - 1:
                dve.wait_ge(bank_done, g * KB)
            elif not first:
                dve.wait_ge(sel_used, (g - 1) * (CH - 1) + c + 1 + CH - SEL_BUFS)
            for t in range(TC):
                last = nc.vector.tensor_scalar(sel[:, c % SEL_BUFS, t], adj_raw[:, b, t], 1.0,
                                               down[:, TC * c + t:TC * c + t + 1],
                                               ALU.is_equal, ALU.mult)
            last.then_inc(sel_made, 1)
            if c == 0:
                if not first:
                    dve.wait_ge(counted, g)
                nc.vector.tensor_scalar(count[:], adj_raw[:, b], 1.0, None, ALU.is_equal).then_inc(chunk_counted, 1)
            else:
                dve.wait_ge(chunk_counted, g * CH + c)
                nc.vector.scalar_tensor_tensor(count[:].rearrange("p t i -> p (t i)"), adj_raw[:, b].rearrange("p t i -> p (t i)"), 1.0,
                                               count[:].rearrange("p t i -> p (t i)"),
                                               ALU.is_equal, ALU.add).then_inc(chunk_counted, 1)

        def scale_x(dve, n, count, i):
            c, t = n // TC, n % TC
            ts = slice(n, n + count)
            nc.vector.tensor_reduce(row_max[:, ts], x_raw[:, c % 2, t:t + count], AX.X, ALU.max,
                                    apply_absolute_value=True).then_inc(x_step, 1)
            dve.wait_ge(x_step, 4 * i + 1)
            nc.vector.tensor_scalar(expo[:, ts], row_max[:, ts].bitcast(I32), 23, None,
                                    ALU.logical_shift_right).then_inc(x_step, 1)
            dve.wait_ge(x_step, 4 * i + 2)
            nc.vector.tensor_scalar(expo_dn[:, ts], expo[:, ts], 15.0, -14.0, ALU.max, ALU.add).then_inc(x_step, 1)
            dve.wait_ge(x_step, 4 * i + 3)
            nc.vector.tensor_scalar(expo[:, ts], expo_dn[:, ts], -1.0, 254.0, ALU.mult, ALU.add).then_inc(x_step, 1)
            dve.wait_ge(x_step, 4 * i + 4)
            nc.vector.tensor_scalar(up[:, ts].bitcast(I32), expo[:, ts], 23, None,
                                    ALU.logical_shift_left).then_inc(scale_made, count)
            nc.vector.tensor_scalar(down[:, ts].bitcast(I32), expo_dn[:, ts], 23, None,
                                    ALU.logical_shift_left).then_inc(unscale_made, count)

        def edge_index(dve):
            dve.wait_ge(pairs_in, 16)
            s, o = pair_sb[:, :, 0], pair_sb[:, :, 1]
            lg, lp, lt = GC.bit_length() - 1, P.bit_length() - 1, (NT * GC).bit_length() - 1
            SHR, SHL, AND, OR = ALU.logical_shift_right, ALU.logical_shift_left, ALU.bitwise_and, ALU.bitwise_or
            nc.vector.tensor_scalar(index_part[:, 0], s, lg, lp + lt, SHR, SHL)
            nc.vector.tensor_scalar(index_part[:, 1], o, P - 1, lt, AND, SHL)
            nc.vector.tensor_scalar(index_part[:, 2], o, lp, lg, SHR, SHL)
            nc.vector.tensor_scalar(adj_index[:], s, GC - 1, None, AND)
            nc.vector.tensor_tensor(off_diag[:], s, o, ALU.not_equal)
            for i in range(3):
                dve.drain()
                last = nc.vector.tensor_tensor(adj_index[:], adj_index[:], index_part[:, i], OR)
            last.then_inc(index_made, 1)

        def edge_counts(dve):
            dve.wait_ge(staged, ET // STAGE)
            nc.vector.scalar_tensor_tensor(live[:], adj_val[:], 1.0, off_diag[:], ALU.is_equal, ALU.mult)
            dve.wait_ge(tables_made, 6)
            nc.vector.tensor_copy(seq[:], seq_i[:])
            dve.drain()
            nc.vector.tensor_tensor_scan(live_sum[:], unit[:], live[:], 0.0, ALU.mult, ALU.add)
            dve.drain()
            nc.vector.tensor_copy(live_total[:], live_sum[:, ET - 1:ET]).then_inc(total_made, 1)

        def edge_slots(dve):
            dve.wait_ge(base_made, 1)
            nc.vector.tensor_copy(base_total[:], ps_b[:, 0:2])
            dve.drain()
            nc.vector.scalar_tensor_tensor(place[:], live_sum[:], base_total[0:EP, 0:1], live[:], ALU.add, ALU.subtract)
            nc.vector.tensor_scalar(n_i[:], base_total[:, 1:2], float(P - 1), None, ALU.add)
            nc.vector.tensor_scalar(valid[:], seq[:], base_total[:, 1:2], None, ALU.is_lt)
            dve.drain()
            nc.vector.tensor_scalar(n_tiles[:], n_i[:], P.bit_length() - 1, None, ALU.logical_shift_right)
            dve.drain()
            nc.vector.tensor_scalar(n_tiles[:], n_tiles[:], 1.0, None, ALU.max)
            dve.drain()
            nc.vector.scalar_tensor_tensor(slot_f[:], place[:], -NONE, live[:], ALU.add, ALU.mult)
            dve.drain()
            nc.vector.tensor_scalar(slot_f[:], slot_f[:], NONE, None, ALU.add).then_inc(slots_made, 1)

        def edge_list(dve, tiles):
            s, o = pair_sb[:, :, 0], pair_sb[:, :, 1]
            for i, end in enumerate((s, o)):
                nc.vector.tensor_scalar(digits_i[:, :, 2 * i], end, 6, None, ALU.logical_shift_right)
                nc.vector.tensor_scalar(digits_i[:, :, 2 * i + 1], end, 63, None, ALU.bitwise_and)
            nc.vector.tensor_copy(lane[:], lane_i[:])
            nc.vector.memset(src[:], 0.0)
            nc.vector.memset(key[:], 0.0)
            dve.drain()
            nc.vector.tensor_copy(digits[:], digits_i[:])
            dve.drain()
            with dve.Fori(0, tiles) as a:
                nc.vector.tensor_copy(slot_16[:], slot_f[:])
                dve.drain()
                nc.vector.tensor_tensor(chosen, lane[:].unsqueeze(1).to_broadcast([EP, ET, P]),
                                        slot_16[:].unsqueeze(2).to_broadcast([EP, ET, P]), ALU.is_equal)
                dve.drain()
                nc.vector.tensor_scalar(slot_f[:], slot_f[:], -float(P), None, ALU.add).then_inc(chosen_made, 1)
                dve.wait_ge(digits_out, a + 1)
                nc.vector.tensor_copy(end_digits[:], ps_b[:, 0:4])
                dve.drain()
                nc.vector.scalar_tensor_tensor(src[:, bass.ds(a, 1)], end_digits[:, 0:1], 64.0, end_digits[:, 1:2],
                                               ALU.mult, ALU.add)
                nc.vector.scalar_tensor_tensor(key[:, bass.ds(a, 1)], end_digits[:, 2:3], 64.0, end_digits[:, 3:4],
                                               ALU.mult, ALU.add)
                dve.drain()
            nc.vector.tensor_copy(edge_sb[:, :, 0], src[:])
            nc.vector.tensor_copy(edge_sb[:, :, 1], key[:])
            dve.drain()
            nc.vector.memset(att[:], 0.0).then_inc(listed, 1)

        def edge_scores(dve, tiles):
            nc.vector.memset(row_top[:], DIAG_SCORE)
            nc.vector.memset(twins[:], 0.0)
            nc.vector.memset(elders[:], 0.0)
            nc.vector.memset(row_sum[:], 0.0)
            dve.drain()
            nc.vector.scalar_tensor_tensor(src[:], src[:], 1.0, valid[:], ALU.add, ALU.mult)
            dve.drain()
            nc.vector.tensor_scalar(src[:], src[:], -1.0, None, ALU.add)
            dve.drain()
            nc.vector.scalar_tensor_tensor(key[:], src[:], float(N), key[:], ALU.mult, ALU.add)
            dve.wait_ge(weights_in, 64)
            with dve.Fori(0, tiles) as a:
                dve.wait_ge(qk_made, 2 * a + 1)
                nc.vector.tensor_tensor(q_sb, ps_a[:, 0], bq_sb[:], ALU.add)
                dve.wait_ge(qk_made, 2 * a + 2)
                nc.vector.tensor_tensor(k_sb, ps_a[:, 1], bk_sb[:], ALU.add)
                dve.drain()
                nc.vector.tensor_tensor(q_sb, q_sb, k_sb, ALU.mult)
                dve.drain()
                nc.vector.tensor_reduce(tile_top[:, 0:HEADS], q_sb.rearrange("p (h d) -> p h d", h=HEADS), AX.X, ALU.add)
                dve.drain()
                nc.vector.tensor_scalar(att[:, bass.ds(a, 1)].rearrange("p o h -> p (o h)"), tile_top[:, 0:HEADS],
                                        1.0 / float(np.sqrt(DK)), valid[:, bass.ds(a, 1)],
                                        ALU.mult, ALU.mult).then_inc(att_made, 1)

            dve.drain()

        def one(t, a):
            return t[:, bass.ds(a, 1)]

        def heads(t, a):
            return t[:, bass.ds(a, 1)].rearrange("p o h -> p (o h)")

        def edge_maxima(dve, tiles):
            with dve.Fori(0, tiles) as b:
                nc.vector.tensor_copy(field[:, 0:HEADS], heads(att, b))
                nc.vector.tensor_copy(field[:, HEADS:HEADS + 1], one(src, b))
                nc.vector.tensor_copy(field[:, HEADS + 1:HEADS + 2], one(key, b))
                nc.vector.tensor_copy(field[:, HEADS + 2:HEADS + 3], one(seq, b))
                dve.drain()
                nc.vector.tensor_copy(field_out[:], field[:]).then_inc(fields_made, 1)
                dve.wait_ge(spread, b + 1)
                nc.vector.tensor_copy(spread_sb, ps_b[:, 0:3 * P])
                dve.drain()
                with dve.Fori(0, tiles) as a:
                    nc.vector.tensor_scalar(same, spread_sb[:, 0:P], one(src, a), None, ALU.is_equal)
                    nc.vector.tensor_scalar(younger, spread_sb[:, 2 * P:3 * P], one(seq, a), None, ALU.is_lt)
                    dve.drain()
                    nc.vector.tensor_scalar(apart, same, -LOWEST, LOWEST, ALU.mult, ALU.add)
                    nc.vector.scalar_tensor_tensor(pair_out, spread_sb[:, P:2 * P], one(key, a), younger,
                                                   ALU.is_equal, ALU.mult, accum_out=tile_cnt[:, 0:1])
                    nc.vector.scalar_tensor_tensor(pair_att[:, HEADS], same, 1.0, younger,
                                                   ALU.mult, ALU.mult, accum_out=tile_cnt[:, 1:2])
                    dve.drain()
                    for i in range(2):
                        nc.vector.tensor_tensor(pair_att[:, 4 * i:4 * i + 4], ps_a[:, i].rearrange("p (h e) -> p h e", e=P),
                                                apart.unsqueeze(1).to_broadcast([P, 4, P]), ALU.add)
                    nc.vector.tensor_tensor(one(twins, a), one(twins, a), tile_cnt[:, 0:1], ALU.add)
                    nc.vector.tensor_tensor(one(elders, a), one(elders, a), tile_cnt[:, 1:2], ALU.add)
                    dve.drain()
                    nc.vector.tensor_reduce(tile_top[:, 0:HEADS], pair_att[:, 0:HEADS], AX.X, ALU.max)
                    dve.drain()
                    nc.vector.tensor_tensor(heads(row_top, a), heads(row_top, a), tile_top[:, 0:HEADS], ALU.max)
                    dve.drain()
            nc.vector.scalar_tensor_tensor(once[:], twins[:], 0.0, valid[:], ALU.is_equal, ALU.mult)
            nc.vector.scalar_tensor_tensor(rep[:], elders[:], 0.0, valid[:], ALU.is_equal, ALU.mult)
            nc.vector.tensor_tensor(p_edge[:, :, 0:HEADS], att[:], row_top[:], ALU.subtract)
            nc.vector.tensor_scalar(p_zero[:], row_top[:], -1.0, None, ALU.mult)
            nc.vector.tensor_scalar(p_diag[:], row_top[:], -1.0, DIAG_SCORE, ALU.mult, ALU.add).then_inc(exp_in, 1)
            dve.drain()
            nc.vector.scalar_tensor_tensor(out_slot_f[:], src[:], -NONE, rep[:], ALU.add, ALU.mult)
            dve.drain()
            nc.vector.tensor_scalar(out_slot[:], out_slot_f[:], NONE, None, ALU.add)

        def edge_sums(dve, tiles):
            dve.wait_ge(exp_made, 1)
            nc.vector.tensor_copy(p_edge[:, :, HEADS], once[:])
            nc.vector.tensor_tensor(p_edge[:, :, 0:HEADS], p_edge[:, :, 0:HEADS],
                                    once[:].unsqueeze(2).to_broadcast([P, ET, HEADS]), ALU.mult)
            dve.drain()
            with dve.Fori(0, tiles) as a:
                nc.vector.tensor_copy(field_out[:, 0:1], one(src, a)).then_inc(row_field, 1)
                dve.wait_ge(row_spread, a + 1)
                nc.vector.tensor_copy(spread_sb[:, 0:P], ps_b[:, 0:P])
                dve.drain()
                with dve.Fori(0, tiles) as b:
                    n = a * tiles + b
                    nc.vector.tensor_scalar(pair_out, spread_sb[:, 0:P], one(src, b), None, ALU.is_equal)
                    dve.drain()
                    nc.vector.tensor_copy(p_field[:], heads(p_edge, b)).then_inc(sum_ready, 1)
                    dve.wait_ge(sum_done, n + 1)
                    nc.vector.tensor_tensor(heads(row_sum, a), heads(row_sum, a), ps_b[:, P:P + HEADS + 1], ALU.add)
                    dve.drain()

        def edge_weights(dve, tiles):
            with dve.Fori(0, tiles) as a:
                dve.wait_ge(nd_in, 16 * a + 16)
                nc.vector.tensor_copy(head_tmp[:, 0], heads(p_zero, a))
                nc.vector.tensor_copy(head_tmp[:, 1], heads(p_diag, a))
                nc.vector.tensor_copy(head_tmp9[:], heads(p_edge, a))
                nc.vector.tensor_copy(tile_top[:], heads(row_sum, a))
                dve.drain()
                nc.vector.tensor_tensor(n_free[:], nd[:, 0:1], tile_top[:, HEADS:HEADS + 1], ALU.subtract)
                nc.vector.tensor_tensor(head_tmp[:, 2], head_tmp[:, 1], tile_top[:, 0:HEADS], ALU.add)
                dve.drain()
                nc.vector.scalar_tensor_tensor(z_head[:], head_tmp[:, 0], n_free[:], head_tmp[:, 2], ALU.mult, ALU.add)
                dve.drain()
                nc.vector.reciprocal(iz_head[:], z_head[:])
                dve.drain()
                mean = 1.0 / HEADS
                nc.vector.scalar_tensor_tensor(z_head[:], head_tmp[:, 0], mean, iz_head[:], ALU.mult, ALU.mult,
                                               accum_out=w_tmp[:, 0:1])
                nc.vector.scalar_tensor_tensor(head_tmp[:, 2], head_tmp[:, 1], mean, iz_head[:], ALU.mult, ALU.mult,
                                               accum_out=w_tmp[:, 1:2])
                nc.vector.scalar_tensor_tensor(tile_top[:, 0:HEADS], head_tmp9[:, 0:HEADS], mean, iz_head[:], ALU.mult, ALU.mult,
                                               accum_out=w_edge[:, 0:1])
                dve.drain()
                nc.vector.tensor_copy(one(w_zero, a), w_tmp[:, 0:1])
                nc.vector.tensor_tensor(w_edge[:, 1:2], w_tmp[:, 0:1], head_tmp9[:, HEADS:HEADS + 1], ALU.mult)
                nc.vector.tensor_tensor(w_tmp[:, 0:1], w_tmp[:, 0:1], nd[:, 1:2], ALU.mult)
                dve.drain()
                nc.vector.tensor_tensor(one(w_diff, a), w_edge[:, 0:1], w_edge[:, 1:2], ALU.subtract)
                nc.vector.scalar_tensor_tensor(one(w_own, a), w_tmp[:, 1:2], 1.0, w_tmp[:, 0:1], ALU.add,
                                               ALU.subtract).then_inc(nd_used, 1)
            dve.drain()
            nc.vector.memset(fix_sum, 0.0).then_inc(weighed, 1)
            dve.drain()

        def edge_parts(dve, tiles):
            with dve.Fori(0, tiles) as a:
                nc.vector.tensor_copy(field_out[:, 0:1], one(src, a)).then_inc(src_field, 1)
                nc.vector.memset(fix_sum, 0.0)
                dve.wait_ge(src_spread, a + 1)
                nc.vector.tensor_copy(spread_sb[:, 0:P], ps_b[:, 0:P])
                dve.drain()
                with dve.Fori(0, tiles) as b:
                    n = a * tiles + b
                    nc.vector.tensor_scalar(pair_out, spread_sb[:, 0:P], one(src, b), None, ALU.is_equal)
                    dve.wait_ge(obj_in, 16 * n + 16)
                    nc.vector.tensor_scalar(fix, x_obj, one(w_diff, b), None, ALU.mult).then_inc(pair_room, 1)
                    dve.drain()
                    nc.vector.tensor_copy(pair_mark[:], n_free[:]).then_inc(pair_ready, 1)
                    dve.wait_ge(pair_done, n + 1)
                    nc.vector.tensor_tensor(fix_sum, fix_sum, ps_a[:, 0], ALU.add)
                    dve.drain()
                dve.wait_ge(own_in, 16 * a + 16)
                nc.vector.scalar_tensor_tensor(fix_part, x_src, one(w_own, a), fix_sum, ALU.mult,
                                               ALU.add).then_inc(parts_done, 1)
                dve.drain()

        def edge_rows(dve, tiles):
            with dve.Fori(0, tiles) as a:
                dve.wait_ge(part_in, 16 * a + 16)
                dve.wait_ge(g_src_in, 16 * a + 16)
                nc.vector.scalar_tensor_tensor(fix_y, g_src, one(w_zero, a), fix_sum, ALU.mult, ALU.add)
                dve.drain()
                nc.vector.bn_stats(fix_stats[:], fix_y)
                dve.drain()
                nc.vector.tensor_tensor(fix_small[:, 0:1], fix_stats[:, 1:2], fix_stats[:, 4:5], ALU.add)
                nc.vector.tensor_tensor(fix_small[:, 1:2], fix_stats[:, 1:2], fix_stats[:, 4:5], ALU.subtract)
                nc.vector.tensor_tensor(fix_small[:, 2:3], fix_stats[:, 2:3], fix_stats[:, 5:6], ALU.add)
                dve.drain()
                nc.vector.scalar_tensor_tensor(fix_small[:, 3:4], fix_small[:, 1:2], H / 4.0, fix_small[:, 1:2],
                                               ALU.mult, ALU.mult)
                dve.drain()
                nc.vector.tensor_tensor(fix_small[:, 4:5], fix_small[:, 2:3], fix_small[:, 3:4], ALU.add).then_inc(fix_var, 1)
                dve.wait_ge(fix_std, a + 1)
                nc.vector.reciprocal(fix_small[:, 6:7], fix_small[:, 5:6])
                dve.drain()
                nc.vector.scalar_tensor_tensor(fix_small[:, 7:8], fix_small[:, 0:1], -0.5, fix_small[:, 6:7],
                                               ALU.mult, ALU.mult)
                dve.drain()
                nc.vector.tensor_scalar(fix_out, fix_y, fix_small[:, 6:7], fix_small[:, 7:8], ALU.mult,
                                        ALU.add).then_inc(fixed, 1)

        @block.vector
        def _(dve):
            for t in range(TC):
                dve.wait_ge(x_first[t], 16)
                scale_x(dve, t, 1, t)
            dve.wait_ge(unscale_made, TC)
            select_chunk(dve, 0, 0, True)
            dve.wait_ge(x_in[1], 16)
            scale_x(dve, TC, TC, TC)
            for c in range(1, CH):
                dve.wait_ge(unscale_made, TC * (c + 1))
                select_chunk(dve, 0, c, True)
                if c + 1 < CH:
                    dve.wait_ge(x_in[(c + 1) % 2], 16 * ((c + 2) // 2))
                    scale_x(dve, TC * (c + 1), TC, TC + c)
                if c == 1:
                    edge_index(dve)
            dve.wait_ge(diag_in, 16)
            nc.vector.tensor_scalar(diag[:], diag_raw[:], 1.0, None, ALU.is_equal).then_inc(diag_made, 1)
            dve.wait_ge(diag_made, 1)

            def group(g, after={}):
                for c in range(CH):
                    select_chunk(dve, g, c, False)
                    if c == 1:
                        coefficients(dve, g - 1)
                    if c == 3:
                        mix_rows(dve, g - 1)
                    if c == 4:
                        scale_rows(dve, g - 1)
                    if c in after:
                        after[c]()

            group(1)
            with dve.Fori(2, SLOT_GROUP) as g:
                group(g)
            group(SLOT_GROUP, {2: lambda: edge_counts(dve)})
            edge_slots(dve)
            tiles = dve.value_load(n_tiles[0:1, 0:1], min_val=1, max_val=ET)
            group(SLOT_GROUP + 1, {1: lambda: edge_list(dve, tiles)})
            with dve.Fori(SLOT_GROUP + 2, SCORE_GROUP + 1) as g:
                group(g)
            edge_scores(dve, tiles)
            group(SCORE_GROUP + 1, {1: lambda: edge_maxima(dve, tiles), 3: lambda: edge_sums(dve, tiles)})
            with dve.Fori(SCORE_GROUP + 2, GR) as g:
                group(g)
            coefficients(dve, GR - 1)
            edge_weights(dve, tiles)
            edge_parts(dve, tiles)
            for i in range(2):
                mix_rows(dve, GR - 1, KB // 2 * i, KB // 2 * (i + 1), GR - 1 + i)
                scale_rows(dve, GR - 1, KB // 2 * i, KB // 2 * (i + 1), GR - 1 + i)
            edge_rows(dve, tiles)

        @block.scalar
        def _(act):
            for c in range(CH):
                if c:
                    act.wait_ge(scale_made, TC * (c + 1))
                if c >= 2:
                    act.wait_ge(lo_made, TC * (c - 1))
                for t in range(TC):
                    n = TC * c + t
                    if c == 0:
                        act.wait_ge(scale_made, t + 1)
                    nc.scalar.activation(x_scaled[:, c % 2, t], x_raw[:, c % 2, t], ACT.Copy,
                                         scale=up[:, n:n + 1])
                    nc.scalar.activation(x_hi[:, n], x_raw[:, c % 2, t], ACT.Copy,
                                         scale=up[:, n:n + 1]).then_inc(hi_made, 1)

            def finish_rows(act, g, k0, k1, i):
                act.wait_ge(mv_made, i + 1)
                nc.scalar.activation(std[:, k0:k1], sq_sum[:, k0:k1], ACT.Sqrt, bias=eps_col[:],
                                     scale=1.0 / H).then_inc(std_made, 1)
                act.wait_ge(shift_made, i + 1)
                for k in range(k0, k1):
                    nc.scalar.activation(y_row[:, k], y_row[:, k], ACT.Identity, bias=shift[:, k:k + 1],
                                         scale=rstd[:, k:k + 1]).then_inc(out_made, 1)
                act.wait_ge(out_made, KB * g + k1)
                act.dma_start(out_rows[g, :, k0:k1], y_row[:, k0:k1]).then_inc(out_sent, 16)

            def finish_group(act, g, first=False, last=False, between=None):
                if last:
                    act.wait_ge(coef_made, g + 1)
                    act.dma_start(nd_rows[g], nd_row[:]).then_inc(nd_sent, 16)
                    act.wait_ge(xrow_in, 16 * (g + 1))
                    for k in range(KB):
                        nc.scalar.activation(x_row[:, k], x_row[:, k], ACT.Copy,
                                             scale=w_self[:, k:k + 1]).then_inc(xpart_made, 1)
                for k in range(KB):
                    act.wait_ge(bank_done, KB * g + k + 1)
                    if not first and k == 0:
                        act.wait_ge(g_sent, 16 * g)
                        act.wait_ge(y_made, KB * g)
                    nc.scalar.activation(g_row[:, k], ps_g[k][:], ACT.Copy).then_inc(bank_read, 1)
                    if last:
                        act.wait_ge(bank_read, KB * g + k + 1)
                        act.dma_start(g_rows[g, :, k], g_row[:, k]).then_inc(g_sent, 16)
                        if k == KB // 2:
                            finish_rows(act, g, 0, KB // 2, g)
                if between:
                    between()
                if not last:
                    act.wait_ge(coef_made, g + 1)
                    act.dma_start(nd_rows[g], nd_row[:]).then_inc(nd_sent, 16)
                    act.wait_ge(bank_read, KB * (g + 1))
                    act.dma_start(g_rows[g], g_row[:]).then_inc(g_sent, 16)
                    act.wait_ge(xrow_in, 16 * (g + 1))
                    for k in range(KB):
                        nc.scalar.activation(x_row[:, k], x_row[:, k], ACT.Copy,
                                             scale=w_self[:, k:k + 1]).then_inc(xpart_made, 1)
                if last:
                    finish_rows(act, g, KB // 2, KB, g + 1)
                else:
                    finish_rows(act, g, 0, KB, g)

            def exponentials():
                act.wait_ge(exp_in, 1)
                nc.scalar.activation(p_edge[:, :, 0:HEADS], p_edge[:, :, 0:HEADS], ACT.Exp)
                nc.scalar.activation(p_zero[:], p_zero[:], ACT.Exp)
                nc.scalar.activation(p_diag[:], p_diag[:], ACT.Exp).then_inc(exp_made, 1)

            act.wait_ge(consts, 2)
            finish_group(act, 0, first=True)
            with act.Fori(1, SLOT_GROUP + 1) as g:
                finish_group(act, g)
            act.wait_ge(listed, 1)
            act.dma_start(wq_sb, wq_t.rearrange("(c p) h -> p c h", p=P)).then_inc(weights_in, 16)
            act.dma_start(wk_sb, wk_t.rearrange("(c p) h -> p c h", p=P)).then_inc(weights_in, 16)
            act.dma_start(bq_sb[:], bq.partition_broadcast(P)).then_inc(weights_in, 16)
            act.dma_start(bk_sb[:], bk.partition_broadcast(P)).then_inc(weights_in, 16)
            finish_group(act, SLOT_GROUP + 1)
            tiles = act.value_load(n_tiles[0:1, 0:1], min_val=1, max_val=ET)
            with act.Fori(0, tiles) as a:
                act.wait_ge(ends_turned, 2 * a + 1)
                nc.scalar.activation(x_src_t, ps_a[:, 0].rearrange("p (c e) -> p c e", e=P), ACT.Copy).then_inc(turned_read, 1)
                act.wait_ge(ends_turned, 2 * a + 2)
                nc.scalar.activation(x_obj_t, ps_a[:, 1].rearrange("p (c e) -> p c e", e=P), ACT.Copy).then_inc(turned_read, 1)
            finish_group(act, SCORE_GROUP, between=exponentials)
            with act.Fori(SCORE_GROUP + 1, GR - 1) as g:
                finish_group(act, g)
            finish_group(act, GR - 1, last=True)
            with act.Fori(0, tiles) as a:
                act.wait_ge(fix_var, a + 1)
                nc.scalar.activation(fix_small[:, 5:6], fix_small[:, 4:5], ACT.Sqrt, bias=eps_col[:],
                                     scale=1.0 / H).then_inc(fix_std, 1)

        @block.tensor
        def _(pe):
            def multiply_group(pe, g, first=False, between={}, count_at=CH // 2 + 1):
                for c in range(CH):
                    pe.wait_ge(sel_made, g * CH + c + 1)
                    if first and c < CH - 1:
                        for t in range(TC):
                            n = TC * c + t
                            pe.wait_ge(hi_made, n + 1)
                            pe.wait_ge(lo_made, n + 1)
                            for k in range(KB):
                                w = sel[:, c % SEL_BUFS, t, k * P:(k + 1) * P]
                                nc.tensor.matmul(ps_g[k][:], w, x_hi[:, n], start=(n == 0), stop=False)
                                last = nc.tensor.matmul(ps_g[k][:], w, x_lo[:, n], start=False, stop=False)
                        last.then_inc(sel_used, 1)
                        continue
                    if first:
                        pe.wait_ge(hi_made, TC * (c + 1))
                        pe.wait_ge(lo_made, TC * (c + 1))
                    if c == count_at:
                        pe.wait_ge(chunk_counted, g * CH + CH)
                        if first:
                            pe.wait_ge(consts, 1)
                        else:
                            pe.wait_ge(coef_made, g)
                        for k in range(KB):
                            for t in range(TC):
                                last = nc.tensor.matmul(ps_cnt[:, k:k + 1], count[:, t, k * P:(k + 1) * P], ones[:],
                                                        start=(t == 0), stop=(t == TC - 1))
                        last.then_inc(counted, 1)
                    for k in range(KB):
                        if c == 0 and not first:
                            pe.wait_ge(bank_read, KB * (g - 1) + k + 1)
                        for t in range(TC):
                            w = sel[:, c % SEL_BUFS, t, k * P:(k + 1) * P]
                            n = TC * c + t
                            nc.tensor.matmul(ps_g[k][:], w, x_hi[:, n], start=(n == 0), stop=False)
                            last = nc.tensor.matmul(ps_g[k][:], w, x_lo[:, n], start=False, stop=(n == NT - 1))
                        if c == CH - 1:
                            last.then_inc(bank_done, 1)
                    if c < CH - 1:
                        last.then_inc(sel_used, 1)
                    if c in between:
                        between[c]()

            def edge_bases():
                pe.wait_ge(tables_made, 6)
                pe.wait_ge(total_made, 1)
                nc.tensor.matmul(ps_b[:, 0:1], before[:], live_total[:], start=True, stop=True)
                nc.tensor.matmul(ps_b[:, 1:2], all_ones[:], live_total[:], start=True, stop=True).then_inc(base_made, 1)

            def edge_list():
                with pe.Fori(0, tiles) as a:
                    pe.wait_ge(chosen_made, a + 1)
                    for c in range(ET):
                        last = nc.tensor.matmul(ps_b[:, 0:4], chosen[:, c], digits[:, c], start=(c == 0), stop=(c == ET - 1))
                    last.then_inc(digits_out, 1)

            def spread_field(column, dst):
                return nc.tensor.matmul(dst, field_out[:, column:column + 1].to_broadcast([P, P]), ident[:],
                                        start=True, stop=True)

            def edge_products():
                pe.wait_ge(weights_in, 64)
                with pe.Fori(0, tiles) as a:
                    pe.wait_ge(ends_in, 32 * a + 32)
                    for i, ends in enumerate((x_src, x_obj)):
                        for c in range(HC):
                            last = nc.tensor.transpose(ps_a[:, i, c * P:(c + 1) * P], ends[:, c * P:(c + 1) * P], ident[:])
                        last.then_inc(ends_turned, 1)
                    for i, (turned, w) in enumerate(((x_src_t, wq_sb), (x_obj_t, wk_sb))):
                        pe.wait_ge(turned_read, 2 * a + i + 1)
                        for c in range(HC):
                            last = nc.tensor.matmul(ps_a[:, i], turned[:, c], w[:, c], start=(c == 0), stop=(c == HC - 1))
                        last.then_inc(qk_made, 1)

            def edge_spread():
                with pe.Fori(0, tiles) as b:
                    pe.wait_ge(fields_made, b + 1)
                    for h in range(HEADS):
                        spread_field(h, ps_a[:, h // 4, (h % 4) * P:(h % 4 + 1) * P])
                    for i in range(3):
                        last = spread_field(HEADS + i, ps_b[:, i * P:(i + 1) * P])
                    last.then_inc(spread, 1)

            def edge_sums():
                with pe.Fori(0, tiles) as a:
                    pe.wait_ge(row_field, a + 1)
                    spread_field(0, ps_b[:, 0:P]).then_inc(row_spread, 1)
                    with pe.Fori(0, tiles) as b:
                        pe.wait_ge(sum_ready, a * tiles + b + 1)
                        nc.tensor.matmul(ps_b[:, P:P + HEADS + 1], pair_out, p_field[:], start=True,
                                         stop=True).then_inc(sum_done, 1)

            def edge_parts():
                with pe.Fori(0, tiles) as a:
                    pe.wait_ge(src_field, a + 1)
                    spread_field(0, ps_b[:, 0:P]).then_inc(src_spread, 1)
                    with pe.Fori(0, tiles) as b:
                        pe.wait_ge(pair_ready, a * tiles + b + 1)
                        nc.tensor.matmul(ps_a[:, 0], pair_out, fix, start=True, stop=True).then_inc(pair_done, 1)

            multiply_group(pe, 0, first=True, count_at=CH - 1)
            with pe.Fori(1, SLOT_GROUP) as g:
                multiply_group(pe, g)
            multiply_group(pe, SLOT_GROUP, between={1: edge_bases})
            pe.wait_ge(slots_made, 1)
            tiles = pe.value_load(n_tiles[0:1, 0:1], min_val=1, max_val=ET)
            multiply_group(pe, SLOT_GROUP + 1, between={0: edge_list}, count_at=CH - 1)
            multiply_group(pe, SCORE_GROUP, between={CH // 2: edge_products, CH - 2: edge_spread})
            multiply_group(pe, SCORE_GROUP + 1, between={2: edge_sums}, count_at=CH - 1)
            multiply_group(pe, GR - 1, between={CH - 2: edge_parts})


def kernel(x, adj, L0_gnn_rel_pair_index, L0_gnn_Wq, L0_gnn_bq, L0_gnn_Wk, L0_gnn_bk):
    import concourse.bacc as bacc
    from concourse.bass_utils import run_bass_kernel_spmd

    x, adj = np.asarray(x), np.asarray(adj)
    N, H = x.shape
    GC = KB * P
    adj_t = np.ascontiguousarray(adj.reshape(N // GC, GC, N // P, P).transpose(0, 3, 2, 1))
    adj_diag = np.ascontiguousarray(np.diagonal(adj).reshape(N // P, P).T)
    pairs = np.asarray(L0_gnn_rel_pair_index)
    arrays = {"x": x, "adj_t": adj_t, "adj_diag": adj_diag, "pairs": pairs,
              "wq_t": np.ascontiguousarray(np.asarray(L0_gnn_Wq).T), "bq": np.asarray(L0_gnn_bq),
              "wk_t": np.ascontiguousarray(np.asarray(L0_gnn_Wk).T), "bk": np.asarray(L0_gnn_bk)}
    nc = bacc.Bacc("TRN2", target_bir_lowering=False, num_devices=1)
    args = {n: nc.dram_tensor(n, a.shape, mybir.dt.from_np(a.dtype), kind="ExternalInput").ap() for n, a in arrays.items()}
    out = nc.dram_tensor("out", (N, H), F32, kind="ExternalOutput").ap()
    scratch = {"g_table": ((N, H), F32), "nd_table": ((N, 2), F32),
               "part_table": ((edge_columns(pairs.shape[0]), P, H), F32)}
    scratch = {n: nc.dram_tensor(n, s, t, kind="Internal").ap() for n, (s, t) in scratch.items()}
    build(nc, *args.values(), out, *scratch.values())
    r = run_bass_kernel_spmd(nc, [arrays], core_ids=[0])
    return r.results[0]["out"]
```

```python
from contextlib import ExitStack

import numpy as np
import concourse.bass as bass
from concourse import mybir

ALU = mybir.AluOpType
ACT = mybir.ActivationFunctionType
AX = mybir.AxisListType
F32 = mybir.dt.float32
BF16 = mybir.dt.bfloat16
F16 = mybir.dt.float16
I32 = mybir.dt.int32

P = 128
KB = 4
TC = 4
RAW_BUFS = 4
SLOT_GROUP = 3
SCORE_GROUP = 5
SEL_BUFS = 4
X_BUFS = 3
BY_TILE = 2
BY_PE = 4
HEADS = 8
STAGE = 16
LN_EPS = 1e-5
DIAG_SCORE = 1e-7
NONE = float(2 ** 20)
LOWEST = -1e38
E_OFF = float(np.exp(np.float32(-DIAG_SCORE)))


def edge_columns(E):
    n = -(-E // P)
    while E % n:
        n += 1
    return n


def build(nc, x, adj_t, adj_diag, pairs, wq_t, bq, wk_t, bk, out, g_table, nd_table, part_table):
    N, H = x.shape
    E = pairs.shape[0]
    ET = edge_columns(E)
    EP = E // ET
    DK = H // HEADS
    assert ET % STAGE == 0
    HC = H // P
    NT = N // P
    GR = N // (P * KB)
    GC = KB * P
    CH = NT // TC

    with ExitStack() as ctx:
        def sb(name, shape, dt):
            return ctx.enter_context(nc.sbuf_tensor(name, shape, dt))

        def psum(name, shape, dt):
            return ctx.enter_context(nc.psum_tensor(name, shape, dt))

        def sem(name):
            return ctx.enter_context(nc.semaphore(name))

        x_space = sb("x_space", [P, 4, TC, H], F32)
        x_raw, x_scaled = x_space[:, 0:X_BUFS], x_space[:, X_BUFS]
        x_hi = sb("x_hi", [P, NT, H], F16)
        x_lo = sb("x_lo", [P, NT, H], F16)
        row_max = sb("row_max", [P, NT], F32)
        power = sb("power", [P, NT], F32)
        up = sb("up", [P, NT], F32)
        up_16 = sb("up_16", [P, BY_PE * TC], BF16)
        down = sb("down", [P, NT], F32)
        adj_raw = sb("adj_raw", [P, RAW_BUFS, TC, GC], F32)
        sel = sb("sel", [P, SEL_BUFS, TC, GC], BF16)
        count = sb("count", [P, TC, GC], BF16)
        ones = sb("ones", [P, 1], BF16)
        diag_raw = sb("diag_raw", [P, NT], F32)
        diag = sb("diag", [P, NT], F32)
        z_row = sb("z_row", [P, KB], F32)
        inv_z = sb("inv_z", [P, KB], F32)
        w_off = sb("w_off", [P, KB], F32)
        w_d = sb("w_d", [P, KB], F32)
        w_self = sb("w_self", [P, KB], F32)
        x_row = sb("x_row", [P, KB, H], F32)
        g_row = sb("g_row", [P, KB, H], F32)
        nd_row = sb("nd_row", [P, KB, 2], F32)
        y_row = sb("y_row", [P, KB, H], F32)
        stats = sb("stats", [P, KB, 6], F32)
        mean = sb("mean", [P, KB], F32)
        gap = sb("gap", [P, KB], F32)
        gap_sq = sb("gap_sq", [P, KB], F32)
        var = sb("var", [P, KB], F32)
        sq_sum = sb("sq_sum", [P, KB], F32)
        std = sb("std", [P, KB], F32)
        rstd = sb("rstd", [P, KB], F32)
        shift = sb("shift", [P, KB], F32)
        eps_col = sb("eps_col", [P, 1], F32)

        pair_sb = sb("pair_sb", [EP, ET, 2], I32)
        adj_index = sb("adj_index", [EP, ET], I32)
        index_part = sb("index_part", [EP, 3, ET], I32)
        digits_i = sb("digits_i", [EP, ET, 4], I32)
        digits = sb("digits", [EP, ET, 4], BF16)
        lane_i = sb("lane_i", [EP, P], I32)
        lane = sb("lane", [EP, P], BF16)
        end_digits = sb("end_digits", [P, 4], F32)
        p_field = sb("p_field", [P, HEADS + 1], F32)
        adj_val = sb("adj_val", [EP, ET], F32)
        off_diag = sb("off_diag", [EP, ET], F32)
        live = sb("live", [EP, ET], F32)
        unit = sb("unit", [EP, ET], F32)
        live_sum = sb("live_sum", [EP, ET], F32)
        live_total = sb("live_total", [EP, 1], BF16)
        before = sb("before", [EP, P], BF16)
        all_ones = sb("all_ones", [EP, P], BF16)
        base_total = sb("base_total", [P, 2], F32)
        place = sb("place", [EP, ET], F32)
        slot_f = sb("slot_f", [EP, ET], F32)
        slot_16 = sb("slot_16", [EP, ET], BF16)
        n_i = sb("n_i", [P, 1], I32)
        n_tiles = sb("n_tiles", [P, 1], I32)
        edge_sb = sb("edge_sb", [P, ET + 1, 2], I32)
        seq_i = sb("seq_i", [P, ET], I32)
        seq = sb("seq", [P, ET], F32)
        valid = sb("valid", [P, ET], F32)
        src_wide = sb("src_wide", [P, ET + 1], F32)
        src = src_wide[:, 0:ET]
        key = sb("key", [P, ET], F32)
        att = sb("att", [P, ET, HEADS], F32)
        row_top = sb("row_top", [P, ET, HEADS], F32)
        twins = sb("twins", [P, ET], F32)
        elders = sb("elders", [P, ET], F32)
        once = sb("once", [P, ET], F32)
        rep = sb("rep", [P, ET], F32)
        p_edge = sb("p_edge", [P, ET, HEADS + 1], F32)
        p_zero = sb("p_zero", [P, ET, HEADS], F32)
        p_diag = sb("p_diag", [P, ET, HEADS], F32)
        row_sum = sb("row_sum", [P, ET, HEADS + 1], F32)
        w_diff = sb("w_diff", [P, ET], F32)
        w_zero = sb("w_zero", [P, ET], F32)
        w_own = sb("w_own", [P, ET], F32)
        out_slot_f = sb("out_slot_f", [P, ET], F32)
        out_slot = sb("out_slot", [P, ET], I32)
        ident = sb("ident", [P, P], F32)
        bq_sb = sb("bq_sb", [P, H], F32)
        bk_sb = sb("bk_sb", [P, H], F32)
        field = sb("field", [P, HEADS + 3], F32)
        field_out = sb("field_out", [P, HEADS + 3], F32)
        head_tmp9 = sb("head_tmp9", [P, HEADS + 1], F32)
        adj_stage = sb("adj_stage", [EP, STAGE], F32)
        pair_mark = sb("pair_mark", [P, 1], F32)
        stage = sb("stage", [EP, STAGE], I32)
        ends = sb("ends", [P, 2], I32)
        obj_ends = sb("obj_ends", [P, 2], I32)
        row_index = sb("row_index", [P, 1], I32)
        tile_top = sb("tile_top", [P, HEADS + 1], F32)
        tile_cnt = sb("tile_cnt", [P, 2], F32)
        nd = sb("nd", [P, 2], F32)
        n_free = sb("n_free", [P, 1], F32)
        z_head = sb("z_head", [P, HEADS], F32)
        iz_head = sb("iz_head", [P, HEADS], F32)
        head_tmp = sb("head_tmp", [P, 3, HEADS], F32)
        w_edge = sb("w_edge", [P, 2], F32)
        w_tmp = sb("w_tmp", [P, 2], F32)
        fix_stats = sb("fix_stats", [P, 6], F32)
        fix_small = sb("fix_small", [P, 8], F32)

        wq_sb, wk_sb = x_space[:, 2], x_space[:, 3]
        x_src, x_obj = x_space[:, 0, 0], x_space[:, 0, 1]
        x_src_t = x_space[:, 0, 2].rearrange("p (c e) -> p c e", e=P)
        x_obj_t = x_space[:, 0, 3].rearrange("p (c e) -> p c e", e=P)
        q_sb, k_sb = x_space[:, 1, 0], x_space[:, 1, 1]
        fix, fix_sum = x_space[:, 1, 2], x_space[:, 1, 3]
        fix_part, fix_y = q_sb, k_sb
        chosen = x_space[:].rearrange("p b t h -> p (b t h)")[0:EP, 0:ET * P // 2].bitcast(BF16).rearrange("p (c j) -> p c j", j=P)
        pair_space = x_space[:, 2].rearrange("p t h -> p (t h)")
        pair_att = pair_space[:, 0:(HEADS + 1) * P].rearrange("p (h e) -> p h e", e=P)
        spread_sb = pair_space[:, (HEADS + 1) * P:(HEADS + 4) * P]
        same, younger, apart, pair_out = (pair_space[:, (HEADS + i) * P:(HEADS + i + 1) * P] for i in (4, 5, 6, 7))
        g_src, fix_out = x_space[:, 3, 0], x_space[:, 3, 1]
        assert HC == TC and H == HC * P

        ps_a = psum("ps_a", [P, 2, H], F32)
        ps_b = psum("ps_b", [P, H], F32)
        ps_g = [psum(f"ps_g{k}", [P, H], F32) for k in range(KB)]
        ps_cnt = psum("ps_cnt", [P, H], F32)

        adj_in = [sem(f"adj_in{b}") for b in range(RAW_BUFS)]
        x_in = [sem(f"x_in{b}") for b in range(X_BUFS)]
        x_first = [sem(f"x_first{t}") for t in range(BY_TILE * TC)]
        adj_first = [sem(f"adj_first{t}") for t in range(BY_TILE * TC)]
        diag_in = sem("diag_in")
        tile_selected = sem("tile_selected")
        sel_made = sem("sel_made")
        chunk_counted = sem("chunk_counted")
        count_made = sem("count_made")
        sel_used = sem("sel_used")
        scale_made = sem("scale_made")
        hi_made = sem("hi_made")
        scaled_made = sem("scaled_made")
        lo_made = sem("lo_made")
        consts = sem("consts")
        x_step = sem("x_step")
        coef_step = sem("coef_step")
        join_step = sem("join_step")
        rstd_made = sem("rstd_made")
        diag_made = sem("diag_made")
        counted = sem("counted")
        coef_made = sem("coef_made")
        bank_done = sem("bank_done")
        bank_read = sem("bank_read")
        xrow_in = sem("xrow_in")
        xpart_made = sem("xpart_made")
        y_made = sem("y_made")
        stats_made = sem("stats_made")
        mv_made = sem("mv_made")
        std_made = sem("std_made")
        unscale_made = sem("unscale_made")
        shift_made = sem("shift_made")
        out_made = sem("out_made")
        out_sent = sem("out_sent")
        g_sent = sem("g_sent")

        pairs_in = sem("pairs_in")
        weights_in = sem("weights_in")
        index_made = sem("index_made")
        adj_val_in = sem("adj_val_in")
        tables_made = sem("tables_made")
        cleared = sem("cleared")
        total_made = sem("total_made")
        base_made = sem("base_made")
        slots_made = sem("slots_made")
        listed = sem("listed")
        chosen_made = sem("chosen_made")
        digits_out = sem("digits_out")
        row_field = sem("row_field")
        row_spread = sem("row_spread")
        sum_ready = sem("sum_ready")
        sum_done = sem("sum_done")
        ends_in = sem("ends_in")
        ends_turned = sem("ends_turned")
        turned_read = sem("turned_read")
        qk_made = sem("qk_made")
        att_made = sem("att_made")
        fields_made = sem("fields_made")
        spread = sem("spread")
        exp_in = sem("exp_in")
        exp_made = sem("exp_made")
        nd_sent = sem("nd_sent")
        nd_in = sem("nd_in")
        nd_used = sem("nd_used")
        src_field = sem("src_field")
        src_spread = sem("src_spread")
        own_in = sem("own_in")
        g_src_in = sem("g_src_in")
        obj_in = sem("obj_in")
        pair_ready = sem("pair_ready")
        pair_done = sem("pair_done")
        fix_var = sem("fix_var")
        fix_std = sem("fix_std")
        fixed = sem("fixed")
        pair_room = sem("pair_room")
        fix_sent = sem("fix_sent")
        staged = sem("staged")
        parts_done = sem("parts_done")
        part_sent = sem("part_sent")
        part_in = sem("part_in")

        x_tiles = x.rearrange("(c t p) h -> c p t h", p=P, t=TC)
        adj_chunks = adj_t.rearrange("g p (c t) i -> g c p t i", t=TC)
        x_rows = x.rearrange("(g k p) h -> g p k h", p=P, k=KB)
        out_rows = out.rearrange("(g k p) h -> g p k h", p=P, k=KB)
        nd_rows = nd_table.rearrange("(g k p) c -> g p k c", p=P, k=KB)
        adj_flat = adj_t.rearrange("g p t (i o) -> (g p t i) o", o=1)
        g_rows = g_table.rearrange("(g k p) h -> g p k h", p=P, k=KB)

        assert SCORE_GROUP + 2 == GR - 1 and SLOT_GROUP + 2 == SCORE_GROUP
        block = ctx.enter_context(nc.Block())

        @block.sync
        def _(sp):
            def load_adj(g, c, wait):
                b = c % RAW_BUFS
                if wait:
                    sp.wait_ge(chunk_counted, g * CH + c + 1 - RAW_BUFS)
                sp.dma_start(adj_raw[:, b], adj_chunks[g, c]).then_inc(adj_in[b], 16)

            for c in range(CH):
                if c >= X_BUFS:
                    sp.wait_ge(scaled_made, TC * (c + 1 - X_BUFS))
                if c < BY_TILE:
                    for t in range(TC):
                        sp.dma_start(x_raw[:, c, t], x_tiles[c, :, t]).then_inc(x_first[TC * c + t], 16)
                        sp.dma_start(adj_raw[:, c, t], adj_chunks[0, c, :, t]).then_inc(adj_first[TC * c + t], 16)
                else:
                    sp.dma_start(x_raw[:, c % X_BUFS], x_tiles[c]).then_inc(x_in[c % X_BUFS], 16)
                    load_adj(0, c, c >= RAW_BUFS)
                if c == 1:
                    sp.dma_start(pair_sb[:], pairs.rearrange("(p t) c -> p t c", t=ET)).then_inc(pairs_in, 16)
                    sp.dma_start(diag_raw[:], adj_diag).then_inc(diag_in, 16)
            sp.dma_start(x_row[:], x_rows[0]).then_inc(xrow_in, 16)
            with sp.Fori(1, GR) as g:
                for c in range(CH):
                    load_adj(g, c, True)
                    if c == CH - 2:
                        sp.wait_ge(y_made, KB * g)
                        sp.dma_start(x_row[:], x_rows[g]).then_inc(xrow_in, 16)

        @block.gpsimd
        def _(pool):
            nc.gpsimd.memset(ones[:], 1.0).then_inc(consts, 1)
            nc.gpsimd.memset(eps_col[:], LN_EPS).then_inc(consts, 1)
            nc.gpsimd.memset(unit[:], 1.0).then_inc(tables_made, 1)
            nc.gpsimd.memset(all_ones[:], 1.0).then_inc(tables_made, 1)
            nc.gpsimd.memset(before[:], 1.0).then_inc(cleared, 1)
            nc.gpsimd.memset(ident[:], 0.0).then_inc(cleared, 1)
            pool.wait_ge(cleared, 2)
            nc.gpsimd.affine_select(out=before[:], in_=before[:], compare_op=ALU.is_gt, fill=0.0, base=0,
                                    pattern=[[1, P]], channel_multiplier=-1).then_inc(tables_made, 1)
            nc.gpsimd.affine_select(out=ident[:], in_=ident[:], compare_op=ALU.not_equal, fill=1.0, base=0,
                                    pattern=[[1, P]], channel_multiplier=-1).then_inc(tables_made, 1)
            nc.gpsimd.iota(seq_i[:], pattern=[[P, ET]], base=0, channel_multiplier=1).then_inc(tables_made, 1)
            nc.gpsimd.iota(lane_i[:], pattern=[[1, P]], base=0, channel_multiplier=0).then_inc(tables_made, 1)

            def adj_of_edges(pool, c):
                pool.indirect_dma_start(
                    out=adj_stage[:, c:c + 1], out_offset=None, in_=adj_flat,
                    in_offset=bass.IndirectOffsetOnAxis(ap=stage[:, c:c + 1], axis=0)).then_inc(adj_val_in, 16)

            for n in range(NT):
                pool.wait_ge(hi_made, n + 1)
                pool.wait_ge(scaled_made, n + 1)
                nc.gpsimd.tensor_tensor(x_lo[:, n], x_scaled[:, n % TC], x_hi[:, n], ALU.subtract).then_inc(lo_made, 1)
            pool.wait_ge(index_made, 1)
            pool.sem_inc(att_made, 1)
            pool.sem_inc(nd_used, 1)
            pool.sem_inc(pair_room, 1)
            with pool.Fori(0, ET // STAGE) as r:
                nc.gpsimd.tensor_copy(stage[:], adj_index[:, bass.ds(r * STAGE, STAGE)])
                pool.drain()
                for c in range(STAGE):
                    adj_of_edges(pool, c)
                pool.wait_ge(adj_val_in, 16 * STAGE * r + 16 * STAGE)
                nc.gpsimd.tensor_copy(adj_val[:, bass.ds(r * STAGE, STAGE)], adj_stage[:]).then_inc(staged, 1)
            pool.wait_ge(listed, 1)
            tiles = pool.value_load(n_tiles[0:1, 0:1], min_val=1, max_val=ET)

            def gather(dst, table, end, ends=ends):
                return pool.indirect_dma_start(
                    out=dst, out_offset=None, in_=table,
                    in_offset=bass.IndirectOffsetOnAxis(ap=ends[:, end:end + 1], axis=0))

            def next_ends(a):
                nc.gpsimd.tensor_copy(ends[:], edge_sb[:, bass.ds(a + 1, 1)].rearrange("p o c -> p (o c)"))
                pool.drain()

            with pool.Fori(0, tiles) as a:
                pool.wait_ge(att_made, a + 1)
                nc.gpsimd.tensor_copy(ends[:], edge_sb[:, bass.ds(a, 1)].rearrange("p o c -> p (o c)"))
                pool.drain()
                gather(x_src, x, 0).then_inc(ends_in, 16)
                gather(x_obj, x, 1).then_inc(ends_in, 16)
                pool.drain()
            pool.wait_ge(nd_sent, 16 * GR)
            with pool.Fori(0, tiles) as a:
                pool.wait_ge(nd_used, a + 1)
                nc.gpsimd.tensor_copy(ends[:], edge_sb[:, bass.ds(a, 1)].rearrange("p o c -> p (o c)"))
                pool.drain()
                gather(nd[:], nd_table, 0).then_inc(nd_in, 16)
                pool.drain()
            nc.gpsimd.tensor_copy(ends[:], edge_sb[:, 0])
            pool.drain()
            with pool.Fori(0, tiles) as a:
                gather(x_src, x, 0).then_inc(own_in, 16)
                with pool.Fori(0, tiles) as b:
                    n = a * tiles + b
                    pool.wait_ge(pair_room, n + 1)
                    nc.gpsimd.tensor_copy(obj_ends[:], edge_sb[:, bass.ds(b, 1)].rearrange("p o c -> p (o c)"))
                    pool.drain()
                    gather(x_obj, x, 1, obj_ends).then_inc(obj_in, 16)
                    pool.drain()
                pool.wait_ge(parts_done, a + 1)
                pool.dma_start(part_table[bass.ds(a, 1)].rearrange("o p h -> p (o h)"), fix_part).then_inc(part_sent, 16)
                pool.wait_ge(part_sent, 16 * a + 16)
                next_ends(a)
            nc.gpsimd.tensor_copy(ends[:], edge_sb[:, 0])
            pool.drain()
            with pool.Fori(0, tiles) as a:
                pool.dma_start(fix_sum, part_table[bass.ds(a, 1)].rearrange("o p h -> p (o h)")).then_inc(part_in, 16)
                pool.wait_ge(g_sent, 16 * (GR - 1 + KB))
                gather(g_src, g_table, 0).then_inc(g_src_in, 16)
                pool.wait_ge(fixed, a + 1)
                nc.gpsimd.tensor_copy(row_index[:], out_slot[:, bass.ds(a, 1)])
                pool.drain()
                pool.wait_ge(out_sent, 16 * (GR + 1))
                pool.indirect_dma_start(
                    out=out, out_offset=bass.IndirectOffsetOnAxis(ap=row_index[:], axis=0),
                    in_=fix_out, in_offset=None, bounds_check=N - 1, oob_is_err=False).then_inc(fix_sent, 16)
                pool.wait_ge(fix_sent, 16 * a + 16)
                next_ends(a)

        def coefficients(dve, g):
            dve.wait_ge(counted, g + 1)
            if not (isinstance(g, int) and g == 0):
                dve.wait_ge(nd_sent, 16 * g)
                dve.wait_ge(xpart_made, KB * g)
            d = diag[:, bass.ds(g * KB, KB)]
            step = 5 * g
            nc.vector.tensor_copy(nd_row[:, :, 1], d)
            neighbours = ps_cnt[:, 0:KB]
            if isinstance(g, int) and g == 0:
                neighbours = inv_z[:]
                nc.vector.tensor_reduce(neighbours, ps_cnt[:, 0:(BY_PE + 1) * KB].rearrange("p (c k) -> p k c", k=KB),
                                        AX.X, ALU.add)
                dve.drain()
            nc.vector.tensor_tensor(nd_row[:, :, 0], neighbours, d, ALU.subtract).then_inc(coef_step, 1)
            dve.wait_ge(coef_step, step + 1)
            nc.vector.tensor_scalar(z_row[:], nd_row[:, :, 0], E_OFF, 1.0, ALU.mult, ALU.add).then_inc(coef_step, 1)
            dve.wait_ge(coef_step, step + 2)
            nc.vector.reciprocal(inv_z[:], z_row[:]).then_inc(coef_step, 1)
            dve.wait_ge(coef_step, step + 3)
            nc.vector.tensor_scalar(w_off[:], inv_z[:], E_OFF, None, ALU.mult).then_inc(coef_step, 1)
            dve.wait_ge(coef_step, step + 4)
            nc.vector.tensor_tensor(w_d[:], w_off[:], d, ALU.mult).then_inc(coef_step, 1)
            dve.wait_ge(coef_step, step + 5)
            nc.vector.scalar_tensor_tensor(w_self[:], inv_z[:], 1.0, w_d[:], ALU.add,
                                           ALU.subtract).then_inc(coef_made, 1)

        def mix_rows(dve, g, k0=0, k1=KB, i=None):
            i = g if i is None else i
            ks = slice(k0, k1)
            for k in range(k0, k1):
                dve.wait_ge(bank_read, KB * g + k + 1)
                dve.wait_ge(xpart_made, KB * g + k + 1)
                if k == 0 and not (isinstance(g, int) and g == 0):
                    dve.wait_ge(out_sent, 16 * g)
                nc.vector.scalar_tensor_tensor(y_row[:, k], g_row[:, k], w_off[:, k:k + 1], x_row[:, k],
                                               ALU.mult, ALU.add).then_inc(y_made, 1)
                dve.wait_ge(y_made, KB * g + k + 1)
                nc.vector.bn_stats(stats[:, k], y_row[:, k]).then_inc(stats_made, 1)
            dve.wait_ge(stats_made, KB * g + k1)
            nc.vector.tensor_tensor(mean[:, ks], stats[:, ks, 1], stats[:, ks, 4], ALU.add).then_inc(join_step, 1)
            nc.vector.tensor_tensor(gap[:, ks], stats[:, ks, 1], stats[:, ks, 4], ALU.subtract).then_inc(join_step, 1)
            nc.vector.tensor_tensor(var[:, ks], stats[:, ks, 2], stats[:, ks, 5], ALU.add).then_inc(join_step, 1)
            dve.wait_ge(join_step, 4 * i + 2)
            nc.vector.scalar_tensor_tensor(gap_sq[:, ks], gap[:, ks], H / 4.0, gap[:, ks], ALU.mult,
                                           ALU.mult).then_inc(join_step, 1)
            dve.wait_ge(join_step, 4 * i + 4)
            nc.vector.tensor_tensor(sq_sum[:, ks], var[:, ks], gap_sq[:, ks], ALU.add).then_inc(mv_made, 1)

        def scale_rows(dve, g, k0=0, k1=KB, i=None):
            i = g if i is None else i
            ks = slice(k0, k1)
            dve.wait_ge(std_made, i + 1)
            nc.vector.reciprocal(rstd[:, ks], std[:, ks]).then_inc(rstd_made, 1)
            dve.wait_ge(rstd_made, i + 1)
            nc.vector.scalar_tensor_tensor(shift[:, ks], mean[:, ks], -0.5, rstd[:, ks], ALU.mult,
                                           ALU.mult).then_inc(shift_made, 1)

        def select_tile(g, c, t):
            return nc.vector.tensor_scalar(sel[:, c % SEL_BUFS, t], adj_raw[:, c % RAW_BUFS, t], 1.0,
                                           down[:, TC * c + t:TC * c + t + 1], ALU.is_equal, ALU.mult)

        def count_chunk(dve, g, c, first):
            b = c % RAW_BUFS
            if first and c < BY_PE:
                dve.wait_ge(sel_made, c + 1)
                nc.vector.tensor_copy(up_16[:, TC * c:TC * (c + 1)], up[:, TC * c:TC * (c + 1)]).then_inc(chunk_counted, 1)
            elif c == (BY_PE if first else 0):
                if not first:
                    dve.wait_ge(counted, g)
                nc.vector.tensor_scalar(count[:], adj_raw[:, b], 1.0, None, ALU.is_equal).then_inc(chunk_counted, 1)
            else:
                dve.wait_ge(chunk_counted, g * CH + c)
                flat = count[:].rearrange("p t i -> p (t i)")
                nc.vector.scalar_tensor_tensor(flat, adj_raw[:, b].rearrange("p t i -> p (t i)"), 1.0, flat,
                                               ALU.is_equal, ALU.add).then_inc(chunk_counted, 1)
            if c == CH - 1:
                half = TC
                while half > 1:
                    half //= 2
                    dve.drain()
                    last = nc.vector.tensor_tensor(count[:, 0:half], count[:, 0:half], count[:, half:2 * half], ALU.add)
                last.then_inc(count_made, 1)

        def select_chunk(dve, g, c, first):
            b = c % RAW_BUFS
            dve.wait_ge(adj_in[b], (g * (CH // RAW_BUFS) + c // RAW_BUFS + (0 if b < BY_TILE else 1)) * 16)
            if c >= SEL_BUFS:
                dve.wait_ge(sel_used, g * (CH - 1) + c + 1 - SEL_BUFS)
            elif not first and c == SEL_BUFS - 1:
                dve.wait_ge(bank_done, g * KB)
            elif not first:
                dve.wait_ge(sel_used, (g - 1) * (CH - 1) + c + 1 + CH - SEL_BUFS)
            for t in range(TC):
                last = select_tile(g, c, t)
            last.then_inc(sel_made, 1)
            count_chunk(dve, g, c, first)

        def scale_x(dve, n, count, i):
            c, t = n // TC, n % TC
            ts = slice(n, n + count)
            nc.vector.tensor_reduce(row_max[:, ts], x_raw[:, c % X_BUFS, t:t + count], AX.X, ALU.max,
                                    apply_absolute_value=True).then_inc(x_step, 1)
            dve.wait_ge(x_step, 2 * i + 1)
            nc.vector.tensor_scalar(power[:, ts].bitcast(I32), row_max[:, ts].bitcast(I32), 0x7f800000, None,
                                    ALU.bitwise_and).then_inc(x_step, 1)
            dve.wait_ge(x_step, 2 * i + 2)
            nc.vector.tensor_scalar(down[:, ts], power[:, ts], 2.0 ** -112, 2.0 ** -14, ALU.max,
                                    ALU.mult).then_inc(unscale_made, count)
            dve.wait_ge(unscale_made, n + count)
            nc.vector.tensor_scalar(up[:, ts].bitcast(I32), down[:, ts].bitcast(I32), -1.0, float(254 << 23), ALU.mult,
                                    ALU.add).then_inc(scale_made, count)

        def edge_index(dve):
            dve.wait_ge(pairs_in, 16)
            s, o = pair_sb[:, :, 0], pair_sb[:, :, 1]
            lg, lp, lt = GC.bit_length() - 1, P.bit_length() - 1, (NT * GC).bit_length() - 1
            SHR, SHL, AND, OR = ALU.logical_shift_right, ALU.logical_shift_left, ALU.bitwise_and, ALU.bitwise_or
            nc.vector.tensor_scalar(index_part[:, 0], s, lg, lp + lt, SHR, SHL)
            nc.vector.tensor_scalar(index_part[:, 1], o, P - 1, lt, AND, SHL)
            nc.vector.tensor_scalar(index_part[:, 2], o, lp, lg, SHR, SHL)
            nc.vector.tensor_scalar(adj_index[:], s, GC - 1, None, AND)
            nc.vector.tensor_tensor(off_diag[:], s, o, ALU.not_equal)
            for i in range(3):
                dve.drain()
                last = nc.vector.tensor_tensor(adj_index[:], adj_index[:], index_part[:, i], OR)
            last.then_inc(index_made, 1)

        def edge_counts(dve):
            dve.wait_ge(staged, ET // STAGE)
            nc.vector.scalar_tensor_tensor(live[:], adj_val[:], 1.0, off_diag[:], ALU.is_equal, ALU.mult)
            dve.wait_ge(tables_made, 6)
            nc.vector.tensor_copy(seq[:], seq_i[:])
            dve.drain()
            nc.vector.tensor_tensor_scan(live_sum[:], unit[:], live[:], 0.0, ALU.mult, ALU.add)
            dve.drain()
            nc.vector.tensor_copy(live_total[:], live_sum[:, ET - 1:ET]).then_inc(total_made, 1)

        def edge_slots(dve):
            dve.wait_ge(base_made, 1)
            nc.vector.tensor_copy(base_total[:], ps_b[:, 0:2])
            dve.drain()
            nc.vector.scalar_tensor_tensor(place[:], live_sum[:], base_total[0:EP, 0:1], live[:], ALU.add, ALU.subtract)
            nc.vector.tensor_scalar(n_i[:], base_total[:, 1:2], float(P - 1), None, ALU.add)
            nc.vector.tensor_scalar(valid[:], seq[:], base_total[:, 1:2], None, ALU.is_lt)
            dve.drain()
            nc.vector.tensor_scalar(n_tiles[:], n_i[:], P.bit_length() - 1, None, ALU.logical_shift_right)
            dve.drain()
            nc.vector.tensor_scalar(n_tiles[:], n_tiles[:], 1.0, None, ALU.max)
            dve.drain()
            nc.vector.scalar_tensor_tensor(slot_f[:], place[:], -NONE, live[:], ALU.add, ALU.mult)
            dve.drain()
            nc.vector.tensor_scalar(slot_f[:], slot_f[:], NONE, None, ALU.add).then_inc(slots_made, 1)

        def edge_list(dve, tiles):
            s, o = pair_sb[:, :, 0], pair_sb[:, :, 1]
            for i, end in enumerate((s, o)):
                nc.vector.tensor_scalar(digits_i[:, :, 2 * i], end, 6, None, ALU.logical_shift_right)
                nc.vector.tensor_scalar(digits_i[:, :, 2 * i + 1], end, 63, None, ALU.bitwise_and)
            nc.vector.tensor_copy(lane[:], lane_i[:])
            nc.vector.memset(src_wide[:], 0.0)
            nc.vector.memset(key[:], 0.0)
            dve.drain()
            nc.vector.tensor_copy(digits[:], digits_i[:])
            dve.drain()
            with dve.Fori(0, tiles) as a:
                nc.vector.tensor_copy(slot_16[:], slot_f[:])
                dve.drain()
                nc.vector.tensor_tensor(chosen, lane[:].unsqueeze(1).to_broadcast([EP, ET, P]),
                                        slot_16[:].unsqueeze(2).to_broadcast([EP, ET, P]), ALU.is_equal)
                dve.drain()
                nc.vector.tensor_scalar(slot_f[:], slot_f[:], -float(P), None, ALU.add).then_inc(chosen_made, 1)
                dve.wait_ge(digits_out, a + 1)
                nc.vector.tensor_copy(end_digits[:], ps_b[:, 0:4])
                dve.drain()
                nc.vector.scalar_tensor_tensor(src[:, bass.ds(a, 1)], end_digits[:, 0:1], 64.0, end_digits[:, 1:2],
                                               ALU.mult, ALU.add)
                nc.vector.scalar_tensor_tensor(key[:, bass.ds(a, 1)], end_digits[:, 2:3], 64.0, end_digits[:, 3:4],
                                               ALU.mult, ALU.add)
                dve.drain()
            nc.vector.tensor_copy(edge_sb[:, :, 0], src_wide[:])
            nc.vector.tensor_copy(edge_sb[:, 0:ET, 1], key[:])
            nc.vector.memset(edge_sb[:, ET:ET + 1, 1], 0)
            dve.drain()
            nc.vector.memset(att[:], 0.0).then_inc(listed, 1)

        def edge_scores(dve, tiles):
            nc.vector.memset(row_top[:], DIAG_SCORE)
            nc.vector.memset(twins[:], 0.0)
            nc.vector.memset(elders[:], 0.0)
            nc.vector.memset(row_sum[:], 0.0)
            dve.drain()
            nc.vector.scalar_tensor_tensor(src[:], src[:], 1.0, valid[:], ALU.add, ALU.mult)
            dve.drain()
            nc.vector.tensor_scalar(src[:], src[:], -1.0, None, ALU.add)
            dve.drain()
            nc.vector.scalar_tensor_tensor(key[:], src[:], float(N), key[:], ALU.mult, ALU.add)
            dve.wait_ge(weights_in, 64)
            with dve.Fori(0, tiles) as a:
                dve.wait_ge(qk_made, 2 * a + 1)
                nc.vector.tensor_tensor(q_sb, ps_a[:, 0], bq_sb[:], ALU.add)
                dve.wait_ge(qk_made, 2 * a + 2)
                nc.vector.tensor_tensor(k_sb, ps_a[:, 1], bk_sb[:], ALU.add)
                dve.drain()
                nc.vector.tensor_tensor(q_sb, q_sb, k_sb, ALU.mult)
                dve.drain()
                nc.vector.tensor_reduce(tile_top[:, 0:HEADS], q_sb.rearrange("p (h d) -> p h d", h=HEADS), AX.X, ALU.add)
                dve.drain()
                nc.vector.tensor_scalar(att[:, bass.ds(a, 1)].rearrange("p o h -> p (o h)"), tile_top[:, 0:HEADS],
                                        1.0 / float(np.sqrt(DK)), valid[:, bass.ds(a, 1)],
                                        ALU.mult, ALU.mult).then_inc(att_made, 1)

            dve.drain()

        def one(t, a):
            return t[:, bass.ds(a, 1)]

        def heads(t, a):
            return t[:, bass.ds(a, 1)].rearrange("p o h -> p (o h)")

        def edge_maxima(dve, tiles):
            with dve.Fori(0, tiles) as b:
                nc.vector.tensor_copy(field[:, 0:HEADS], heads(att, b))
                nc.vector.tensor_copy(field[:, HEADS:HEADS + 1], one(src, b))
                nc.vector.tensor_copy(field[:, HEADS + 1:HEADS + 2], one(key, b))
                nc.vector.tensor_copy(field[:, HEADS + 2:HEADS + 3], one(seq, b))
                dve.drain()
                nc.vector.tensor_copy(field_out[:], field[:]).then_inc(fields_made, 1)
                dve.wait_ge(spread, b + 1)
                nc.vector.tensor_copy(spread_sb, ps_b[:, 0:3 * P])
                dve.drain()
                with dve.Fori(0, tiles) as a:
                    nc.vector.tensor_scalar(same, spread_sb[:, 0:P], one(src, a), None, ALU.is_equal)
                    nc.vector.tensor_scalar(younger, spread_sb[:, 2 * P:3 * P], one(seq, a), None, ALU.is_lt)
                    dve.drain()
                    nc.vector.tensor_scalar(apart, same, -LOWEST, LOWEST, ALU.mult, ALU.add)
                    nc.vector.scalar_tensor_tensor(pair_out, spread_sb[:, P:2 * P], one(key, a), younger,
                                                   ALU.is_equal, ALU.mult, accum_out=tile_cnt[:, 0:1])
                    nc.vector.scalar_tensor_tensor(pair_att[:, HEADS], same, 1.0, younger,
                                                   ALU.mult, ALU.mult, accum_out=tile_cnt[:, 1:2])
                    dve.drain()
                    for i in range(2):
                        nc.vector.tensor_tensor(pair_att[:, 4 * i:4 * i + 4], ps_a[:, i].rearrange("p (h e) -> p h e", e=P),
                                                apart.unsqueeze(1).to_broadcast([P, 4, P]), ALU.add)
                    nc.vector.tensor_tensor(one(twins, a), one(twins, a), tile_cnt[:, 0:1], ALU.add)
                    nc.vector.tensor_tensor(one(elders, a), one(elders, a), tile_cnt[:, 1:2], ALU.add)
                    dve.drain()
                    nc.vector.tensor_reduce(tile_top[:, 0:HEADS], pair_att[:, 0:HEADS], AX.X, ALU.max)
                    dve.drain()
                    nc.vector.tensor_tensor(heads(row_top, a), heads(row_top, a), tile_top[:, 0:HEADS], ALU.max)
                    dve.drain()
            nc.vector.scalar_tensor_tensor(once[:], twins[:], 0.0, valid[:], ALU.is_equal, ALU.mult)
            nc.vector.scalar_tensor_tensor(rep[:], elders[:], 0.0, valid[:], ALU.is_equal, ALU.mult)
            nc.vector.tensor_tensor(p_edge[:, :, 0:HEADS], att[:], row_top[:], ALU.subtract)
            nc.vector.tensor_scalar(p_zero[:], row_top[:], -1.0, None, ALU.mult)
            nc.vector.tensor_scalar(p_diag[:], row_top[:], -1.0, DIAG_SCORE, ALU.mult, ALU.add).then_inc(exp_in, 1)
            dve.drain()
            nc.vector.scalar_tensor_tensor(out_slot_f[:], src[:], -NONE, rep[:], ALU.add, ALU.mult)
            dve.drain()
            nc.vector.tensor_scalar(out_slot[:], out_slot_f[:], NONE, None, ALU.add)

        def offer_sources(dve, a, offered):
            nc.vector.tensor_copy(field_out[:, 0:1], one(src_wide, a)).then_inc(offered, 1)

        def take_sources(dve, a, spread):
            dve.wait_ge(spread, a + 1)
            nc.vector.tensor_copy(spread_sb[:, 0:P], ps_b[:, 0:P])
            dve.drain()

        def edge_sums(dve, tiles):
            dve.wait_ge(exp_made, 1)
            nc.vector.tensor_copy(p_edge[:, :, HEADS], once[:])
            nc.vector.tensor_tensor(p_edge[:, :, 0:HEADS], p_edge[:, :, 0:HEADS],
                                    once[:].unsqueeze(2).to_broadcast([P, ET, HEADS]), ALU.mult)
            dve.drain()
            take_sources(dve, 0, row_spread)
            with dve.Fori(0, tiles) as a:
                offer_sources(dve, a + 1, row_field)
                with dve.Fori(0, tiles) as b:
                    n = a * tiles + b
                    nc.vector.tensor_scalar(pair_out, spread_sb[:, 0:P], one(src, b), None, ALU.is_equal)
                    dve.drain()
                    nc.vector.tensor_copy(p_field[:], heads(p_edge, b)).then_inc(sum_ready, 1)
                    dve.wait_ge(sum_done, n + 1)
                    nc.vector.tensor_tensor(heads(row_sum, a), heads(row_sum, a), ps_b[:, P:P + HEADS + 1], ALU.add)
                    dve.drain()
                take_sources(dve, a + 1, row_spread)

        def edge_weights(dve, tiles):
            with dve.Fori(0, tiles) as a:
                dve.wait_ge(nd_in, 16 * a + 16)
                nc.vector.tensor_copy(head_tmp[:, 0], heads(p_zero, a))
                nc.vector.tensor_copy(head_tmp[:, 1], heads(p_diag, a))
                nc.vector.tensor_copy(head_tmp9[:], heads(p_edge, a))
                nc.vector.tensor_copy(tile_top[:], heads(row_sum, a))
                dve.drain()
                nc.vector.tensor_tensor(n_free[:], nd[:, 0:1], tile_top[:, HEADS:HEADS + 1], ALU.subtract)
                nc.vector.tensor_tensor(head_tmp[:, 2], head_tmp[:, 1], tile_top[:, 0:HEADS], ALU.add)
                dve.drain()
                nc.vector.scalar_tensor_tensor(z_head[:], head_tmp[:, 0], n_free[:], head_tmp[:, 2], ALU.mult, ALU.add)
                dve.drain()
                nc.vector.reciprocal(iz_head[:], z_head[:])
                dve.drain()
                mean = 1.0 / HEADS
                nc.vector.scalar_tensor_tensor(z_head[:], head_tmp[:, 0], mean, iz_head[:], ALU.mult, ALU.mult,
                                               accum_out=w_tmp[:, 0:1])
                nc.vector.scalar_tensor_tensor(head_tmp[:, 2], head_tmp[:, 1], mean, iz_head[:], ALU.mult, ALU.mult,
                                               accum_out=w_tmp[:, 1:2])
                nc.vector.scalar_tensor_tensor(tile_top[:, 0:HEADS], head_tmp9[:, 0:HEADS], mean, iz_head[:], ALU.mult, ALU.mult,
                                               accum_out=w_edge[:, 0:1])
                dve.drain()
                nc.vector.tensor_copy(one(w_zero, a), w_tmp[:, 0:1])
                nc.vector.tensor_tensor(w_edge[:, 1:2], w_tmp[:, 0:1], head_tmp9[:, HEADS:HEADS + 1], ALU.mult)
                nc.vector.tensor_tensor(w_tmp[:, 0:1], w_tmp[:, 0:1], nd[:, 1:2], ALU.mult)
                dve.drain()
                nc.vector.tensor_tensor(one(w_diff, a), w_edge[:, 0:1], w_edge[:, 1:2], ALU.subtract)
                nc.vector.scalar_tensor_tensor(one(w_own, a), w_tmp[:, 1:2], 1.0, w_tmp[:, 0:1], ALU.add,
                                               ALU.subtract).then_inc(nd_used, 1)
            dve.drain()

        def edge_parts(dve, tiles):
            take_sources(dve, 0, src_spread)
            with dve.Fori(0, tiles) as a:
                offer_sources(dve, a + 1, src_field)
                nc.vector.memset(fix_sum, 0.0)
                dve.drain()
                with dve.Fori(0, tiles) as b:
                    n = a * tiles + b
                    nc.vector.tensor_scalar(pair_out, spread_sb[:, 0:P], one(src, b), None, ALU.is_equal)
                    dve.wait_ge(obj_in, 16 * n + 16)
                    nc.vector.tensor_scalar(fix, x_obj, one(w_diff, b), None, ALU.mult).then_inc(pair_room, 1)
                    dve.drain()
                    nc.vector.tensor_copy(pair_mark[:], n_free[:]).then_inc(pair_ready, 1)
                    dve.wait_ge(pair_done, n + 1)
                    nc.vector.tensor_tensor(fix_sum, fix_sum, ps_a[:, 0], ALU.add)
                    dve.drain()
                dve.wait_ge(own_in, 16 * a + 16)
                nc.vector.scalar_tensor_tensor(fix_part, x_src, one(w_own, a), fix_sum, ALU.mult,
                                               ALU.add).then_inc(parts_done, 1)
                take_sources(dve, a + 1, src_spread)

        def edge_rows(dve, tiles):
            with dve.Fori(0, tiles) as a:
                dve.wait_ge(part_in, 16 * a + 16)
                dve.wait_ge(g_src_in, 16 * a + 16)
                nc.vector.scalar_tensor_tensor(fix_y, g_src, one(w_zero, a), fix_sum, ALU.mult, ALU.add)
                dve.drain()
                nc.vector.bn_stats(fix_stats[:], fix_y)
                dve.drain()
                nc.vector.tensor_tensor(fix_small[:, 0:1], fix_stats[:, 1:2], fix_stats[:, 4:5], ALU.add)
                nc.vector.tensor_tensor(fix_small[:, 1:2], fix_stats[:, 1:2], fix_stats[:, 4:5], ALU.subtract)
                nc.vector.tensor_tensor(fix_small[:, 2:3], fix_stats[:, 2:3], fix_stats[:, 5:6], ALU.add)
                dve.drain()
                nc.vector.scalar_tensor_tensor(fix_small[:, 3:4], fix_small[:, 1:2], H / 4.0, fix_small[:, 1:2],
                                               ALU.mult, ALU.mult)
                dve.drain()
                nc.vector.tensor_tensor(fix_small[:, 4:5], fix_small[:, 2:3], fix_small[:, 3:4], ALU.add).then_inc(fix_var, 1)
                dve.wait_ge(fix_std, a + 1)
                nc.vector.reciprocal(fix_small[:, 6:7], fix_small[:, 5:6])
                dve.drain()
                nc.vector.scalar_tensor_tensor(fix_small[:, 7:8], fix_small[:, 0:1], -0.5, fix_small[:, 6:7],
                                               ALU.mult, ALU.mult)
                dve.drain()
                nc.vector.tensor_scalar(fix_out, fix_y, fix_small[:, 6:7], fix_small[:, 7:8], ALU.mult,
                                        ALU.add).then_inc(fixed, 1)

        @block.vector
        def _(dve):
            for c in range(BY_TILE):
                for t in range(TC):
                    n = TC * c + t
                    dve.wait_ge(x_first[n], 16)
                    scale_x(dve, n, 1, n)
                    dve.wait_ge(adj_first[n], 16)
                    dve.wait_ge(unscale_made, n + 1)
                    select_tile(0, c, t).then_inc(tile_selected if t < TC - 1 else sel_made, 1)
                count_chunk(dve, 0, c, True)
            for c in range(BY_TILE, CH):
                b = c % X_BUFS
                dve.wait_ge(x_in[b], 16 * (c // X_BUFS + (0 if b < BY_TILE else 1)))
                scale_x(dve, TC * c, TC, TC * BY_TILE + c - BY_TILE)
                dve.wait_ge(unscale_made, TC * (c + 1))
                select_chunk(dve, 0, c, True)
                if c == BY_TILE:
                    edge_index(dve)
            dve.wait_ge(diag_in, 16)
            nc.vector.tensor_scalar(diag[:], diag_raw[:], 1.0, None, ALU.is_equal).then_inc(diag_made, 1)
            dve.wait_ge(diag_made, 1)

            def group(g, after={}):
                for c in range(CH):
                    select_chunk(dve, g, c, False)
                    if c == 1:
                        coefficients(dve, g - 1)
                    if c == 3:
                        mix_rows(dve, g - 1)
                    if c == 4:
                        scale_rows(dve, g - 1)
                    if c in after:
                        after[c]()

            group(1)
            with dve.Fori(2, SLOT_GROUP) as g:
                group(g)
            group(SLOT_GROUP, {2: lambda: edge_counts(dve)})
            edge_slots(dve)
            tiles = dve.value_load(n_tiles[0:1, 0:1], min_val=1, max_val=ET)
            group(SLOT_GROUP + 1, {1: lambda: edge_list(dve, tiles)})
            with dve.Fori(SLOT_GROUP + 2, SCORE_GROUP + 1) as g:
                group(g)
            edge_scores(dve, tiles)
            group(SCORE_GROUP + 1, {1: lambda: edge_maxima(dve, tiles),
                                    2: lambda: offer_sources(dve, 0, row_field), 3: lambda: edge_sums(dve, tiles)})
            with dve.Fori(SCORE_GROUP + 2, GR) as g:
                group(g)
            offer_sources(dve, 0, src_field)
            coefficients(dve, GR - 1)
            edge_weights(dve, tiles)
            edge_parts(dve, tiles)
            for i, (k0, k1) in enumerate(((0, KB - 1), (KB - 1, KB))):
                mix_rows(dve, GR - 1, k0, k1, GR - 1 + i)
                scale_rows(dve, GR - 1, k0, k1, GR - 1 + i)
            edge_rows(dve, tiles)

        @block.scalar
        def _(act):
            for c in range(CH):
                if c >= BY_TILE:
                    act.wait_ge(scale_made, TC * (c + 1))
                for t in range(TC):
                    n = TC * c + t
                    if c < BY_TILE:
                        act.wait_ge(scale_made, n + 1)
                    nc.scalar.activation(x_hi[:, n], x_raw[:, c % X_BUFS, t], ACT.Copy,
                                         scale=up[:, n:n + 1]).then_inc(hi_made, 1)
                    if c:
                        act.wait_ge(lo_made, n + 1 - TC)
                    nc.scalar.activation(x_scaled[:, t], x_raw[:, c % X_BUFS, t], ACT.Copy,
                                         scale=up[:, n:n + 1]).then_inc(scaled_made, 1)

            def finish_rows(act, g, k0, k1, i):
                act.wait_ge(mv_made, i + 1)
                nc.scalar.activation(std[:, k0:k1], sq_sum[:, k0:k1], ACT.Sqrt, bias=eps_col[:],
                                     scale=1.0 / H).then_inc(std_made, 1)
                act.wait_ge(shift_made, i + 1)
                for k in range(k0, k1):
                    nc.scalar.activation(y_row[:, k], y_row[:, k], ACT.Identity, bias=shift[:, k:k + 1],
                                         scale=rstd[:, k:k + 1]).then_inc(out_made, 1)

            def send_rows(act, g, k0, k1):
                act.wait_ge(out_made, KB * g + k1)
                act.dma_start(out_rows[g, :, k0:k1], y_row[:, k0:k1]).then_inc(out_sent, 16)

            def finish_group(act, g, first=False, last=False, between=None):
                if last:
                    act.wait_ge(coef_made, g + 1)
                    act.dma_start(nd_rows[g], nd_row[:]).then_inc(nd_sent, 16)
                    act.wait_ge(xrow_in, 16 * (g + 1))
                    for k in range(KB):
                        nc.scalar.activation(x_row[:, k], x_row[:, k], ACT.Copy,
                                             scale=w_self[:, k:k + 1]).then_inc(xpart_made, 1)
                for k in range(KB):
                    act.wait_ge(bank_done, KB * g + k + 1)
                    if not first and k == 0:
                        act.wait_ge(g_sent, 16 * g)
                        act.wait_ge(y_made, KB * g)
                    nc.scalar.activation(g_row[:, k], ps_g[k][:], ACT.Copy).then_inc(bank_read, 1)
                    if last:
                        act.wait_ge(bank_read, KB * g + k + 1)
                        act.dma_start(g_rows[g, :, k], g_row[:, k]).then_inc(g_sent, 16)
                if between:
                    between()
                if not last:
                    act.wait_ge(coef_made, g + 1)
                    act.dma_start(nd_rows[g], nd_row[:]).then_inc(nd_sent, 16)
                    act.wait_ge(bank_read, KB * (g + 1))
                    act.dma_start(g_rows[g], g_row[:]).then_inc(g_sent, 16)
                    act.wait_ge(xrow_in, 16 * (g + 1))
                    for k in range(KB):
                        nc.scalar.activation(x_row[:, k], x_row[:, k], ACT.Copy,
                                             scale=w_self[:, k:k + 1]).then_inc(xpart_made, 1)
                if last:
                    finish_rows(act, g, 0, KB - 1, g)
                    send_rows(act, g, 0, KB - 1)
                    finish_rows(act, g, KB - 1, KB, g + 1)
                    send_rows(act, g, KB - 1, KB)
                else:
                    finish_rows(act, g, 0, KB, g)
                    send_rows(act, g, 0, KB)

            def exponentials():
                act.wait_ge(exp_in, 1)
                nc.scalar.activation(p_edge[:, :, 0:HEADS], p_edge[:, :, 0:HEADS], ACT.Exp)
                nc.scalar.activation(p_zero[:], p_zero[:], ACT.Exp)
                nc.scalar.activation(p_diag[:], p_diag[:], ACT.Exp).then_inc(exp_made, 1)

            act.wait_ge(consts, 2)
            finish_group(act, 0, first=True)
            with act.Fori(1, SLOT_GROUP + 1) as g:
                finish_group(act, g)
            act.wait_ge(listed, 1)
            act.dma_start(wq_sb, wq_t.rearrange("(c p) h -> p c h", p=P)).then_inc(weights_in, 16)
            act.dma_start(wk_sb, wk_t.rearrange("(c p) h -> p c h", p=P)).then_inc(weights_in, 16)
            act.dma_start(bq_sb[:], bq.partition_broadcast(P)).then_inc(weights_in, 16)
            act.dma_start(bk_sb[:], bk.partition_broadcast(P)).then_inc(weights_in, 16)
            finish_group(act, SLOT_GROUP + 1)
            tiles = act.value_load(n_tiles[0:1, 0:1], min_val=1, max_val=ET)
            with act.Fori(0, tiles) as a:
                act.wait_ge(ends_turned, 2 * a + 1)
                nc.scalar.activation(x_src_t, ps_a[:, 0].rearrange("p (c e) -> p c e", e=P), ACT.Copy).then_inc(turned_read, 1)
                act.wait_ge(ends_turned, 2 * a + 2)
                nc.scalar.activation(x_obj_t, ps_a[:, 1].rearrange("p (c e) -> p c e", e=P), ACT.Copy).then_inc(turned_read, 1)
            finish_group(act, SCORE_GROUP, between=exponentials)
            with act.Fori(SCORE_GROUP + 1, GR - 1) as g:
                finish_group(act, g)
            finish_group(act, GR - 1, last=True)
            with act.Fori(0, tiles) as a:
                act.wait_ge(fix_var, a + 1)
                nc.scalar.activation(fix_small[:, 5:6], fix_small[:, 4:5], ACT.Sqrt, bias=eps_col[:],
                                     scale=1.0 / H).then_inc(fix_std, 1)

        @block.tensor
        def _(pe):
            def multiply_group(pe, g, first=False, between={}, count_at=CH - 2, between_banks={}):
                for c in range(CH):
                    if not first or c >= BY_TILE:
                        pe.wait_ge(sel_made, g * CH + c + 1)
                    if first and c < CH - 1:
                        for t in range(TC):
                            n = TC * c + t
                            if c < BY_TILE and t < TC - 1:
                                pe.wait_ge(tile_selected, (TC - 1) * c + t + 1)
                            elif c < BY_TILE:
                                pe.wait_ge(sel_made, c + 1)
                            pe.wait_ge(hi_made, n + 1)
                            for k in range(KB):
                                nc.tensor.matmul(ps_g[k][:], sel[:, c % SEL_BUFS, t, k * P:(k + 1) * P], x_hi[:, n],
                                                 start=(n == 0), stop=False)
                            pe.wait_ge(lo_made, n + 1)
                            for k in range(KB):
                                last = nc.tensor.matmul(ps_g[k][:], sel[:, c % SEL_BUFS, t, k * P:(k + 1) * P],
                                                        x_lo[:, n], start=False, stop=False)
                        if c < BY_PE:
                            pe.wait_ge(chunk_counted, c + 1)
                            for k in range(KB):
                                for t in range(TC):
                                    last = nc.tensor.matmul(ps_cnt[:, (c + 1) * KB + k:(c + 1) * KB + k + 1],
                                                            sel[:, c % SEL_BUFS, t, k * P:(k + 1) * P],
                                                            up_16[:, TC * c + t:TC * c + t + 1],
                                                            start=(t == 0), stop=(t == TC - 1))
                        last.then_inc(sel_used, 1)
                        continue
                    if first:
                        pe.wait_ge(hi_made, TC * (c + 1))
                        pe.wait_ge(lo_made, TC * (c + 1))
                    if c == count_at:
                        pe.wait_ge(count_made, g + 1)
                        if first:
                            pe.wait_ge(consts, 1)
                        else:
                            pe.wait_ge(coef_made, g)
                        for k in range(KB):
                            last = nc.tensor.matmul(ps_cnt[:, k:k + 1], count[:, 0, k * P:(k + 1) * P], ones[:],
                                                    start=True, stop=True)
                        last.then_inc(counted, 1)
                    for k in range(KB):
                        if c == 0 and not first:
                            pe.wait_ge(bank_read, KB * (g - 1) + k + 1)
                        for t in range(TC):
                            w = sel[:, c % SEL_BUFS, t, k * P:(k + 1) * P]
                            n = TC * c + t
                            nc.tensor.matmul(ps_g[k][:], w, x_hi[:, n], start=(n == 0), stop=False)
                            last = nc.tensor.matmul(ps_g[k][:], w, x_lo[:, n], start=False, stop=(n == NT - 1))
                        if c == CH - 1:
                            last.then_inc(bank_done, 1)
                            if k in between_banks:
                                between_banks[k]()
                    if c < CH - 1:
                        last.then_inc(sel_used, 1)
                    if c in between:
                        between[c]()

            def edge_bases():
                pe.wait_ge(tables_made, 6)
                pe.wait_ge(total_made, 1)
                nc.tensor.matmul(ps_b[:, 0:1], before[:], live_total[:], start=True, stop=True)
                nc.tensor.matmul(ps_b[:, 1:2], all_ones[:], live_total[:], start=True, stop=True).then_inc(base_made, 1)

            def edge_list():
                with pe.Fori(0, tiles) as a:
                    pe.wait_ge(chosen_made, a + 1)
                    for c in range(ET):
                        last = nc.tensor.matmul(ps_b[:, 0:4], chosen[:, c], digits[:, c], start=(c == 0), stop=(c == ET - 1))
                    last.then_inc(digits_out, 1)

            def spread_field(column, dst):
                return nc.tensor.matmul(dst, field_out[:, column:column + 1].to_broadcast([P, P]), ident[:],
                                        start=True, stop=True)

            def edge_products():
                pe.wait_ge(weights_in, 64)
                with pe.Fori(0, tiles) as a:
                    pe.wait_ge(ends_in, 32 * a + 32)
                    for i, ends in enumerate((x_src, x_obj)):
                        for c in range(HC):
                            last = nc.tensor.transpose(ps_a[:, i, c * P:(c + 1) * P], ends[:, c * P:(c + 1) * P], ident[:])
                        last.then_inc(ends_turned, 1)
                    for i, (turned, w) in enumerate(((x_src_t, wq_sb), (x_obj_t, wk_sb))):
                        pe.wait_ge(turned_read, 2 * a + i + 1)
                        for c in range(HC):
                            last = nc.tensor.matmul(ps_a[:, i], turned[:, c], w[:, c], start=(c == 0), stop=(c == HC - 1))
                        last.then_inc(qk_made, 1)

            def edge_spread():
                with pe.Fori(0, tiles) as b:
                    pe.wait_ge(fields_made, b + 1)
                    for h in range(HEADS):
                        spread_field(h, ps_a[:, h // 4, (h % 4) * P:(h % 4 + 1) * P])
                    for i in range(3):
                        last = spread_field(HEADS + i, ps_b[:, i * P:(i + 1) * P])
                    last.then_inc(spread, 1)

            def spread_sources(a, offered, spread):
                pe.wait_ge(offered, a + 1)
                spread_field(0, ps_b[:, 0:P]).then_inc(spread, 1)

            def edge_sums():
                with pe.Fori(0, tiles) as a:
                    spread_sources(a + 1, row_field, row_spread)
                    with pe.Fori(0, tiles) as b:
                        pe.wait_ge(sum_ready, a * tiles + b + 1)
                        nc.tensor.matmul(ps_b[:, P:P + HEADS + 1], pair_out, p_field[:], start=True,
                                         stop=True).then_inc(sum_done, 1)

            def edge_parts():
                with pe.Fori(0, tiles) as a:
                    spread_sources(a + 1, src_field, src_spread)
                    with pe.Fori(0, tiles) as b:
                        pe.wait_ge(pair_ready, a * tiles + b + 1)
                        nc.tensor.matmul(ps_a[:, 0], pair_out, fix, start=True, stop=True).then_inc(pair_done, 1)

            multiply_group(pe, 0, first=True, count_at=CH - 1)
            with pe.Fori(1, SLOT_GROUP) as g:
                multiply_group(pe, g)
            multiply_group(pe, SLOT_GROUP, between={1: edge_bases})
            pe.wait_ge(slots_made, 1)
            tiles = pe.value_load(n_tiles[0:1, 0:1], min_val=1, max_val=ET)
            multiply_group(pe, SLOT_GROUP + 1, between={0: edge_list}, count_at=CH - 1)
            multiply_group(pe, SCORE_GROUP, between={CH // 2: edge_products, CH - 2: edge_spread})
            multiply_group(pe, SCORE_GROUP + 1, between={1: lambda: spread_sources(0, row_field, row_spread),
                                                         2: edge_sums}, count_at=CH - 1)
            multiply_group(pe, GR - 1, between={CH // 2: lambda: spread_sources(0, src_field, src_spread)},
                           between_banks={0: edge_parts}, count_at=CH // 2 + 1)


def kernel(x, adj, L0_gnn_rel_pair_index, L0_gnn_Wq, L0_gnn_bq, L0_gnn_Wk, L0_gnn_bk):
    import concourse.bacc as bacc
    from concourse.bass_utils import run_bass_kernel_spmd

    x, adj = np.asarray(x), np.asarray(adj)
    N, H = x.shape
    GC = KB * P
    adj_t = np.ascontiguousarray(adj.reshape(N // GC, GC, N // P, P).transpose(0, 3, 2, 1))
    adj_diag = np.ascontiguousarray(np.diagonal(adj).reshape(N // P, P).T)
    pairs = np.asarray(L0_gnn_rel_pair_index)
    arrays = {"x": x, "adj_t": adj_t, "adj_diag": adj_diag, "pairs": pairs,
              "wq_t": np.ascontiguousarray(np.asarray(L0_gnn_Wq).T), "bq": np.asarray(L0_gnn_bq),
              "wk_t": np.ascontiguousarray(np.asarray(L0_gnn_Wk).T), "bk": np.asarray(L0_gnn_bk)}
    nc = bacc.Bacc("TRN2", target_bir_lowering=False, num_devices=1)
    args = {n: nc.dram_tensor(n, a.shape, mybir.dt.from_np(a.dtype), kind="ExternalInput").ap() for n, a in arrays.items()}
    out = nc.dram_tensor("out", (N, H), F32, kind="ExternalOutput").ap()
    scratch = {"g_table": ((N, H), F32), "nd_table": ((N, 2), F32),
               "part_table": ((edge_columns(pairs.shape[0]), P, H), F32)}
    scratch = {n: nc.dram_tensor(n, s, t, kind="Internal").ap() for n, (s, t) in scratch.items()}
    build(nc, *args.values(), out, *scratch.values())
    r = run_bass_kernel_spmd(nc, [arrays], core_ids=[0])
    return r.results[0]["out"]
```
